# Optimizing a Trainium2 kernel written in Bass

```python
import numpy as np
import jax
import jax.numpy as jnp

def _softmax(x, axis=-1):
    return jax.nn.softmax(x, axis=axis)

def _gelu(x):
    return jax.nn.gelu(x, approximate=True)

def _silu(x):
    return jax.nn.silu(x)

def _sigmoid(x):
    return jax.nn.sigmoid(x)

def _layernorm(x, axis=-1, eps=1e-05):
    m = jnp.mean(x, axis=axis, keepdims=True)
    v = jnp.var(x, axis=axis, keepdims=True)
    return (x - m) / jnp.sqrt(v + eps)

def _scatter_add(tgt, idx, src, axis=0):
    return tgt.at[idx].add(src)

def _segment_sum(src, seg, n):
    return jax.ops.segment_sum(src, seg, n)
kernel_name = 'mk_vit_tower_d1_tok_img1024_r4_a7ff59'

def setup_inputs(seed: int=0):
    np.random.seed(seed)
    _w = jnp.asarray

    def _rec_inputs():
        import jax
        import jax.numpy as jnp
        _rk = jax.random.key(seed)
        x = -0.000222058 + 0.999998 * jax.random.normal(jax.random.fold_in(_rk, 1), (64, 3, 64, 64), jnp.float32)
        return x
    x = _rec_inputs()

    def _L0_tok_setup():
        import jax, jax.numpy as jnp
        import numpy as np
        P = 16
        C = 3
        D = 256

        def _patchify(x, p):
            B, Cc, H, W = x.shape
            gh, gw = (H // p, W // p)
            x = x.reshape(B, Cc, gh, p, gw, p)
            x = x.transpose(0, 2, 4, 1, 3, 5)
            return x.reshape(B, gh * gw, Cc * p * p)
        key = jax.random.key(seed)
        k1, k2, k3, k4, k5 = jax.random.split(key, 5)
        patch_dim = C * P * P
        s1 = 1.0 / np.sqrt(patch_dim)
        s2 = 1.0 / np.sqrt(D)
        return {'x': jax.random.normal(k1, (32, C, 128, 128), dtype=jnp.float32), 'W1': jax.random.uniform(k2, (patch_dim, D), jnp.float32, -s1, s1), 'b1': jax.random.uniform(k3, (D,), jnp.float32, -s1, s1), 'W2': jax.random.uniform(k4, (D, D), jnp.float32, -s2, s2), 'b2': jax.random.uniform(k5, (D,), jnp.float32, -s2, s2)}
    _L0_tok_all = _L0_tok_setup()
    _L0_tok_in = {k: v for k, v in _L0_tok_all.items() if k in ('W1', 'b1', 'W2', 'b2')}
    del _L0_tok_all

    def _L0_attn_setup():
        import jax, jax.numpy as jnp
        import numpy as np
        import math
        B_SZ, L, D, S = (4, 1024, 256, 64)

        def _blelloch_exclusive_scan(a, b):

            def combine(p, q):
                pa, pb = p
                qa, qb = q
                return (pa * qa, pa * qb + pb)
            _, b_inc = jax.lax.associative_scan(combine, (a, b), axis=1)
            return jnp.concatenate([jnp.zeros_like(b_inc[:, :1]), b_inc[:, :-1]], axis=1)
        key = jax.random.key(seed)
        k0, k1, k2, k3 = jax.random.split(key, 4)
        x = jax.random.normal(k0, (B_SZ, L, D), dtype=jnp.float32)
        B_w = jax.random.normal(k1, (S, D), dtype=jnp.float32) * (1.0 / math.sqrt(D))
        C_w = jax.random.normal(k2, (D, S), dtype=jnp.float32) * (1.0 / math.sqrt(S))
        gate_w = jax.random.normal(k3, (D, D), dtype=jnp.float32) * (1.0 / math.sqrt(D))
        gate_b = jnp.zeros((D,), dtype=jnp.float32)
        log_decay = jnp.full((D,), math.log(0.9), dtype=jnp.float32)
        return {'x': x, 'B_w': B_w, 'C_w': C_w, 'gate_w': gate_w, 'gate_b': gate_b, 'log_decay': log_decay}
    _L0_attn_all = _L0_attn_setup()
    _L0_attn_in = {k: v for k, v in _L0_attn_all.items() if k in ('B_w', 'C_w', 'gate_w', 'gate_b', 'log_decay')}
    del _L0_attn_all

    def _L0_ffn_setup():
        import jax, jax.numpy as jnp
        import numpy as np
        key = jax.random.key(seed)
        ks = jax.random.split(key, 6)
        B, L, D, E = (4, 512, 256, 4)
        H = 4 * D
        x = jax.random.normal(ks[0], (B, L, D), dtype=jnp.float32)
        rW1 = jax.random.normal(ks[1], (D, 2 * D), dtype=jnp.float32) * (2.0 / D) ** 0.5
        rb1 = jnp.zeros((2 * D,), dtype=jnp.float32)
        rW2 = jax.random.normal(ks[2], (2 * D, E), dtype=jnp.float32) * (2.0 / (2 * D)) ** 0.5
        rb2 = jnp.zeros((E,), dtype=jnp.float32)
        We1 = jax.random.normal(ks[3], (E, D, H), dtype=jnp.float32) * (2.0 / D) ** 0.5
        be1 = jnp.zeros((E, H), dtype=jnp.float32)
        We2 = jax.random.normal(ks[4], (E, H, D), dtype=jnp.float32) * (2.0 / H) ** 0.5
        be2 = jnp.zeros((E, D), dtype=jnp.float32)
        return {'x': x, 'rW1': rW1, 'rb1': rb1, 'rW2': rW2, 'rb2': rb2, 'We1': We1, 'be1': be1, 'We2': We2, 'be2': be2}
    _L0_ffn_all = _L0_ffn_setup()
    _L0_ffn_in = {k: v for k, v in _L0_ffn_all.items() if k in ('rW1', 'rb1', 'rW2', 'rb2', 'We1', 'be1', 'We2', 'be2')}
    del _L0_ffn_all
    return {'x': x, 'L0_tok_W1': _L0_tok_in['W1'], 'L0_tok_b1': _L0_tok_in['b1'], 'L0_tok_W2': _L0_tok_in['W2'], 'L0_tok_b2': _L0_tok_in['b2'], 'L0_attn_B_w': _L0_attn_in['B_w'], 'L0_attn_C_w': _L0_attn_in['C_w'], 'L0_attn_gate_w': _L0_attn_in['gate_w'], 'L0_attn_gate_b': _L0_attn_in['gate_b'], 'L0_attn_log_decay': _L0_attn_in['log_decay'], 'L0_ffn_rW1': _L0_ffn_in['rW1'], 'L0_ffn_rb1': _L0_ffn_in['rb1'], 'L0_ffn_rW2': _L0_ffn_in['rW2'], 'L0_ffn_rb2': _L0_ffn_in['rb2'], 'L0_ffn_We1': _L0_ffn_in['We1'], 'L0_ffn_be1': _L0_ffn_in['be1'], 'L0_ffn_We2': _L0_ffn_in['We2'], 'L0_ffn_be2': _L0_ffn_in['be2']}

def reference(x, L0_tok_W1, L0_tok_b1, L0_tok_W2, L0_tok_b2, L0_attn_B_w, L0_attn_C_w, L0_attn_gate_w, L0_attn_gate_b, L0_attn_log_decay, L0_ffn_rW1, L0_ffn_rb1, L0_ffn_rW2, L0_ffn_rb2, L0_ffn_We1, L0_ffn_be1, L0_ffn_We2, L0_ffn_be2):
    import jax
    import jax.numpy as jnp

    def _L0_tok_ref(x, W1, b1, W2, b2):
        import jax, jax.numpy as jnp
        import numpy as np
        P = 16
        C = 3
        D = 256

        def _patchify(x, p):
            B, Cc, H, W = x.shape
            gh, gw = (H // p, W // p)
            x = x.reshape(B, Cc, gh, p, gw, p)
            x = x.transpose(0, 2, 4, 1, 3, 5)
            return x.reshape(B, gh * gw, Cc * p * p)
        patches = _patchify(x, P)
        h = jax.nn.silu(jnp.einsum('blk,kd->bld', patches, W1) + b1)
        return jnp.einsum('bld,de->ble', h, W2) + b2

    def _L0_attn_ref(x, B_w, C_w, gate_w, gate_b, log_decay):
        import jax, jax.numpy as jnp
        import numpy as np
        import math
        B_SZ, L, D, S = (4, 1024, 256, 64)

        def _blelloch_exclusive_scan(a, b):

            def combine(p, q):
                pa, pb = p
                qa, qb = q
                return (pa * qa, pa * qb + pb)
            _, b_inc = jax.lax.associative_scan(combine, (a, b), axis=1)
            return jnp.concatenate([jnp.zeros_like(b_inc[:, :1]), b_inc[:, :-1]], axis=1)
        Bu = jnp.einsum('bld,sd->bls', x, B_w)
        Bu_proj = jnp.einsum('bls,ds->bld', Bu, C_w)
        decay = jax.nn.sigmoid(log_decay)
        a = jnp.broadcast_to(decay, Bu_proj.shape)
        h = _blelloch_exclusive_scan(a, Bu_proj)
        gate = jax.nn.sigmoid(jnp.einsum('bld,ed->ble', x, gate_w) + gate_b)
        return gate * h

    def _L0_ffn_ref(x, rW1, rb1, rW2, rb2, We1, be1, We2, be2):
        import jax, jax.numpy as jnp
        import numpy as np
        E = We1.shape[0]
        top_k = min(2, E)
        rh = jax.nn.gelu(x @ rW1 + rb1, approximate=False)
        router_logits = rh @ rW2 + rb2
        router_probs = jax.nn.softmax(router_logits, axis=-1)
        expert_weights, expert_indices = jax.lax.top_k(router_probs, top_k)
        one_hot = jax.nn.one_hot(expert_indices, E, dtype=x.dtype)
        token_mask = one_hot.sum(axis=2)
        combine_w = (one_hot * expert_weights[..., None]).sum(axis=2)
        out = jnp.zeros_like(x)
        for e in range(E):
            xi = x * token_mask[..., e:e + 1]
            h = jax.nn.gelu(xi @ We1[e] + be1[e], approximate=False)
            yo = h @ We2[e] + be2[e]
            out = out + yo * combine_w[..., e:e + 1]
        return out
    h = _L0_tok_ref(x, L0_tok_W1, L0_tok_b1, L0_tok_W2, L0_tok_b2)
    h = h + _L0_attn_ref(_layernorm(h, axis=-1), L0_attn_B_w, L0_attn_C_w, L0_attn_gate_w, L0_attn_gate_b, L0_attn_log_decay)
    h = h + _L0_ffn_ref(_layernorm(h, axis=-1), L0_ffn_rW1, L0_ffn_rb1, L0_ffn_rW2, L0_ffn_rb2, L0_ffn_We1, L0_ffn_be1, L0_ffn_We2, L0_ffn_be2)
    return h

_drawn_inputs = setup_inputs


def setup_inputs(seed=0):
    import zlib

    import numpy as np

    out = dict(_drawn_inputs(seed))
    spreads = {'L0_attn_gate_b': (0.0, 0.1),
     'L0_attn_log_decay': (-0.10536051541566849, 0.2),
     'L0_ffn_rb1': (0.0, 0.1),
     'L0_ffn_rb2': (0.0, 0.1),
     'L0_ffn_be1': (0.0, 0.1),
     'L0_ffn_be2': (0.0, 0.1)}
    factors = {}
    for name, (base, spread) in spreads.items():
        noise = np.random.default_rng([zlib.crc32(name.encode()), seed]).standard_normal(out[name].shape)
        drawn = base * np.exp(spread * noise) if base else spread * noise
        out[name] = jnp.asarray(drawn.astype(out[name].dtype))
    for name, factor in factors.items():
        out[name] = (out[name] * factor).astype(out[name].dtype)
    return out
```

```python
import concourse.bass as bass
from concourse import mybir

TOKENS, D, KP, S, R, E, HID = 1024, 256, 768, 64, 512, 4, 1024
SEQ = 16
P = 128
G = TOKENS // P
HT = TOKENS // 2
DC, KC, RC, HC = D // P, KP // P, R // P, HID // P
TOPK = 2
NT = (TOPK * TOKENS + E * (P - 1)) // P
NTP = NT + 1
EPS = 1e-5

C_IDENT, C_IOTA, C_TRI, C_ONES = 0, 128, 256, 384
C_THR19 = 512
C_IOTA20 = C_THR19 + NT
C_THR8 = C_IOTA20 + NTP
C_TOK1 = C_THR8 + G
C_PAD = C_TOK1 + G
C_TRI4 = C_PAD + 1
C_RESET = C_TRI4 + E * E
C_NEGHALF = C_RESET + E * G
C_COLS = C_NEGHALF + G
V_B1, V_GB, V_LD, V_RB1, V_RW2 = 0, DC, 2 * DC, 3 * DC, 3 * DC + RC
V_COLS = V_RW2 + RC * E


def tower(nc, xT, w1, w2, b2, bw, cw, gw, rw1, rb2, we1, be1, we2, be2, vecs, consts, out):
    f32, f32r, i32 = mybir.dt.float32, mybir.dt.float32r, mybir.dt.int32
    ALU = mybir.AluOpType
    ACT = mybir.ActivationFunctionType
    AX = mybir.AxisListType

    BASE = 16512
    KB = 1024

    def place(name, shape, at, dt=f32):
        return nc.alloc_sbuf_tensor_at(name, [P] + shape, dt, offset=BASE + int(at * KB))

    w1e_hi = place("w1e_hi", [E, DC, HID], 0, f32r)
    w1e_raw = place("w1e_raw", [E, DC, HID], 32)
    w1e_lo = place("w1e_lo", [E, DC, HID], 32, f32r)
    w2e_hi = place("w2e_hi", [E, HC, D], 64, f32r)
    w2e_raw = place("w2e_raw", [E, HC, D], 96)
    w2e_lo = place("w2e_lo", [E, HC, D], 96, f32r)
    x_hi = place("x_hi", [KC, TOKENS], 64, f32r)
    w1_hi = place("w1_hi", [KC, D], 88, f32r)
    x_raw = place("x_raw", [KC, TOKENS], 96)
    x_lo = place("x_lo", [KC, TOKENS], 96, f32r)
    w1_raw = place("w1_raw", [KC, D], 120)
    w1_lo = place("w1_lo", [KC, D], 120, f32r)
    scan_out = place("scan_out", [DC, TOKENS], 64)
    bu_hi = place("bu_hi", [TOKENS], 80, f32r)
    bu_lo = place("bu_lo", [TOKENS], 84, f32r)
    gate = place("gate", [DC, TOKENS], 88)
    rh = place("rh", [RC, TOKENS], 64)
    be1_bc = place("be1_bc", [E, HID], 128)
    be2_bc = place("be2_bc", [E, D], 144)
    b2_bc = place("b2_bc", [D], 148)
    cst = place("cst", [C_COLS], 149)
    vec = place("vec", [V_COLS], 151.75)
    rb2_bc = place("rb2_bc", [E], 151.875)
    decay = place("decay", [DC], 151.90625)
    stats = place("stats", [G, 6], 151.9375)
    mv = place("mv", [G, 2], 152.125)
    veps = place("veps", [G], 152.1875)
    rstd = place("rstd", [G], 152.21875)
    e_of_tile = place("e_of_tile", [NTP], 152.25, i32)
    gather_idx = place("gather_idx", [NTP], 152.34375, i32)
    scatter_idx = place("scatter_idx", [NTP], 152.4375, i32)
    slot_w = place("slot_w", [NTP], 152.53125)
    rw1_hi = place("rw1_hi", [DC, R], 152.75, f32r)
    rw1_raw = place("rw1_raw", [DC, R], 156.75)
    rw1_lo = place("rw1_lo", [DC, R], 156.75, f32r)
    gw_hi = place("gw_hi", [DC, D], 160.75, f32r)
    gw_raw = place("gw_raw", [DC, D], 162.75)
    gw_lo = place("gw_lo", [DC, D], 162.75, f32r)
    w2_hi = place("w2_hi", [DC, D], 164.75, f32r)
    w2_raw = place("w2_raw", [DC, D], 166.75)
    w2_lo = place("w2_lo", [DC, D], 166.75, f32r)
    cw_hi = place("cw_hi", [D], 168.75, f32r)
    cw_raw = place("cw_raw", [D], 169.75)
    cw_lo = place("cw_lo", [D], 169.75, f32r)
    bw_st = place("bw_st", [DC, 2 * S], 170.75, f32r)
    bw_raw = place("bw_raw", [DC, S], 206.75)
    h = place("h", [G, D], 171.75)
    xn = place("xn", [G, D], 179.75)
    h1_hi = place("h1_hi", [DC, TOKENS], 187.75, f32r)
    h1_raw = place("h1_raw", [DC, TOKENS], 195.75)
    h1_lo = place("h1_lo", [DC, TOKENS], 195.75, f32r)
    xT_hi = place("xT_hi", [DC, TOKENS], 187.75, f32r)
    xT_lo = place("xT_lo", [DC, TOKENS], 195.75, f32r)
    carry = place("carry", [HT], 64 + 8)
    powers = place("powers", [DC, SEQ], 64 + 10)
    zero = place("zero", [D], 205.75)
    RT = 152.75
    lg = place("lg", [G, E], RT)
    lmax = place("lmax", [G], RT + .125)
    lsum = place("lsum", [G], RT + .15625)
    lrec = place("lrec", [G], RT + .1875)
    ex = place("ex", [G, E], RT + .25)
    pr = place("pr", [G, E], RT + .375)
    beats = place("beats", [G, E, E], RT + .5)
    ties = place("ties", [G, E, E], RT + 1)
    rank = place("rank", [G, E], RT + 1.5)
    mask = place("mask", [E, G], RT + 1.625)
    incl = place("incl", [E, G], RT + 1.75)
    full = place("full", [E, G], RT + 1.875)
    ntile = place("ntile", [E], RT + 2)
    tincl = place("tincl", [E], RT + 2.03125)
    tstart = place("tstart", [E], RT + 2.0625)
    reach = place("reach", [NTP, E - 1], RT + 2.125)
    e_f = place("e_f", [NTP], RT + 2.375)
    pos = place("pos", [E, G], RT + 2.5)
    selpos = place("selpos", [E, G], RT + 2.625)
    isb = place("isb", [E, G], RT + 2.75)
    isa = place("isa", [E, G], RT + 2.875)
    psum2 = place("psum2", [G], RT + 3)
    pos2 = place("pos2", [2, G], RT + 3.0625)
    slot2 = place("slot2", [2, G], RT + 3.125)
    w2s = place("w2s", [2, G], RT + 3.1875)
    hi2 = place("hi2", [2 * G], RT + 3.25)
    lo2 = place("lo2", [2 * G], RT + 3.3125)
    vals = place("vals", [2 * G, 3], RT + 3.375)
    wtmp = place("wtmp", [E, G], RT + 3.5625)
    thr_ge = place("thr_ge", [2 * G, NT], RT + 3.75)
    oh_hi = place("oh_hi", [2 * G, NTP], RT + 5)
    tab_rhs = place("tab_rhs", [2 * G, 3, NTP], RT + 6.25, f32r)
    oh_lo = place("oh_lo", [2 * G, P], RT + 10, f32r)
    tab = place("tab", [3, NTP], RT + 18)
    padz = place("padz", [NTP], RT + 18.25)
    y = place("y", [2, D], 171.75)
    y_w = place("y_w", [2, D], 173.75)
    xg_hi = place("xg_hi", [2, DC, P], 175.75, f32r)
    xg_lo = place("xg_lo", [2, DC, P], 177.75, f32r)
    hpre = place("hpre", [2, HID], 179.75)
    hT_hi = place("hT_hi", [2, HC, P], 187.75, f32r)
    hT_raw = place("hT_raw", [2, HC, P], 195.75)
    hT_lo = place("hT_lo", [2, HC, P], 195.75, f32r)
    xg = place("xg", [2, D], 203.75)

    xn_rows = nc.dram_tensor("xn_rows", [TOKENS, D], f32, kind="Internal").ap()

    bank = [nc.alloc_psum_tensor(f"bank{i}", [P, 512], f32) for i in range(8)]

    def sem(name):
        return nc.alloc_semaphore(name)

    x_in = [sem(f"x_in{k}") for k in range(KC)]
    small_in, mid_in, be_in = sem("small_in"), sem("mid_in"), sem("be_in")
    w1e_in = [sem(f"w1e_in{e}") for e in range(E)]
    w2e_in = [sem(f"w2e_in{e}") for e in range(E)]
    x_hi_ok, x_ok = sem("x_hi_ok"), sem("x_ok")
    wsm_hi_ok, wsm_ok = sem("wsm_hi_ok"), sem("wsm_ok")
    w1e_hi_ok, w1e_ok = sem("w1e_hi_ok"), sem("w1e_ok")
    w2e_hi_ok, w2e_ok = sem("w2e_hi_ok"), sem("w2e_ok")
    embed_done, silu_done, h1_ok = sem("embed_done"), sem("silu_done"), sem("h1_ok")
    tok_done, h_ok = sem("tok_done"), sem("h_ok")
    veps_ok, rstd_ok, xn_ok = sem("veps_ok"), sem("rstd_ok"), sem("xn_ok")
    xnT_done, xT_hi_ok, xT_ok = sem("xnT_done"), sem("xT_hi_ok"), sem("xT_ok")
    bu_done, bu_hi_ok, bu_ok = sem("bu_done"), sem("bu_hi_ok"), sem("bu_ok")
    gate_done, gate_ok, decay_ok = sem("gate_done"), sem("gate_ok"), sem("decay_ok")
    c_done, attn_ok, attnT_done, h2_ok = sem("c_done"), sem("attn_ok"), sem("attnT_done"), sem("h2_ok")
    router_done, rh_ok, logits_done = sem("router_done"), sem("rh_ok"), sem("logits_done")
    shifted_ok, exp_ok, mask_ok, counts_done = sem("shifted_ok"), sem("exp_ok"), sem("mask_ok"), sem("counts_done")
    onehot_ok, table_done, emap_ok, idx_ok = sem("onehot_ok"), sem("table_done"), sem("emap_ok"), sem("idx_ok")
    xn_stored, h2_stored, zero_ok = sem("xn_stored"), sem("h2_stored"), sem("zero_ok")
    gathered = [sem("gathered0"), sem("gathered1")]
    xgT_done, xg_hi_ok, xg_ok = sem("xgT_done"), sem("xg_hi_ok"), sem("xg_ok")
    up_done, hpre_ok, hT_done = sem("up_done"), sem("hpre_ok"), sem("hT_done")
    gelu_ok, hT_ok, down_done = sem("gelu_ok"), sem("hT_ok"), sem("down_done")
    y_ok, yw_ok, scattered = sem("y_ok"), sem("yw_ok"), sem("scattered")
    dve_step = sem("dve_step")

    ident = cst[:, C_IDENT:C_IDENT + P]

    def half(k):
        return slice(k * HT, (k + 1) * HT)

    def rows(g):
        return slice(g * P, (g + 1) * P)

    def bf(ap):
        return ap.bitcast(f32)

    FULL = range(4, 18)

    with nc.Block() as block:

        @block.sync
        def _(sp):
            for k in range(KC):
                sp.dma_start(x_raw[:, k, :], xT[k, :, :]).then_inc(x_in[k], 16)
                sp.dma_start(w1_raw[:, k, :], w1[k * P:(k + 1) * P, :]).then_inc(x_in[k], 16)
            for e in range(E):
                sp.dma_start(w1e_raw[:, e], we1[e].rearrange("(c p) n -> p c n", p=P)).then_inc(w1e_in[e], 16)
            sp.dma_start(be1_bc[:, :, :], be1.partition_broadcast(P)).then_inc(be_in, 16)
            sp.dma_start(be2_bc[:, :, :], be2.partition_broadcast(P)).then_inc(be_in, 16)
            sp.wait_ge(embed_done, 2 * DC)
            for e in range(E):
                sp.dma_start(w2e_raw[:, e], we2[e].rearrange("(c p) n -> p c n", p=P)).then_inc(w2e_in[e], 16)
            sp.wait_ge(zero_ok, 1)
            sp.dma_start(out[TOKENS:TOKENS + P, :], zero[:, :]).then_inc(h2_stored, 16)
            for k in range(2):
                gs = slice(4 * k, 4 * k + 4)
                sp.wait_ge(h2_ok, 4 * (k + 1))
                sp.dma_start(out[half(k), :].rearrange("(g p) n -> p g n", p=P), h[:, gs, :]).then_inc(h2_stored, 16)
                sp.wait_ge(xn_ok, G + 4 * (k + 1))
                sp.dma_start(xn_rows[half(k), :].rearrange("(g p) n -> p g n", p=P), xn[:, gs, :]).then_inc(xn_stored, 16)

        @block.gpsimd
        def _(pool):
            pool.dma_start(vec[:, :], vecs[:, :]).then_inc(small_in, 16)
            pool.dma_start(cst[:, :], consts[:, :]).then_inc(small_in, 16)
            pool.dma_start(b2_bc[:, :], b2.partition_broadcast(P)).then_inc(small_in, 16)
            pool.dma_start(rb2_bc[:, :], rb2.partition_broadcast(P)).then_inc(small_in, 16)
            pool.dma_start(w2_raw[:, :, :], w2.rearrange("(c p) n -> p c n", p=P)).then_inc(small_in, 16)
            pool.dma_start(bw_raw[:, :, :], bw.rearrange("(c p) n -> p c n", p=P)).then_inc(mid_in, 16)
            pool.dma_start(cw_raw[0:S, :], cw[:, :]).then_inc(mid_in, 16)
            pool.dma_start(cw_raw[S:2 * S, :], cw[:, :]).then_inc(mid_in, 16)
            pool.dma_start(gw_raw[:, :, :], gw.rearrange("(c p) n -> p c n", p=P)).then_inc(mid_in, 16)
            pool.dma_start(rw1_raw[:, :, :], rw1.rearrange("(c p) n -> p c n", p=P)).then_inc(mid_in, 16)
            nc.gpsimd.memset(zero[:, :], 0.0).then_inc(zero_ok, 1)

            def inverse_deviation(n):
                k = n % 2
                pool.wait_ge(veps_ok, n + 1)
                nc.gpsimd.tensor_tensor(rstd[:, 4 * k:4 * k + 4], veps[:, 4 * k:4 * k + 4],
                                        cst[:, C_NEGHALF:C_NEGHALF + 4], ALU.pow).then_inc(rstd_ok, 1)

            def low_part(e):
                pool.wait_ge(w1e_hi_ok, e + 1)
                nc.gpsimd.tensor_tensor(w1e_lo[:, e], w1e_raw[:, e], bf(w1e_hi[:, e]), ALU.subtract).then_inc(w1e_ok, 1)

            pool.wait_ge(small_in, 80)
            inverse_deviation(0)
            inverse_deviation(1)
            low_part(0)
            low_part(1)
            inverse_deviation(2)
            inverse_deviation(3)
            low_part(2)
            low_part(3)

            pool.wait_ge(idx_ok, 1)
            pool.wait_ge(xn_stored, 32)

            def gather(j):
                if j >= NT:
                    return
                if j >= 2:
                    pool.wait_ge(gathered[j % 2], 16 * (j // 2))
                    pool.wait_ge(xgT_done, j - 1)
                nc.gpsimd.indirect_dma_start(
                    out=xg[:, j % 2, :], out_offset=None, in_=xn_rows[:, :],
                    in_offset=bass.IndirectOffsetOnAxis(ap=gather_idx[:, j:j + 1], axis=0),
                ).then_inc(gathered[j % 2], 16)

            for j in range(5):
                gather(j)
            pool.wait_ge(h2_stored, 48)
            for j in range(NT):
                gather(j + 5)
                if j >= 1:
                    pool.wait_ge(scattered, 16 * j)
                pool.wait_ge(yw_ok, j + 1)
                nc.gpsimd.indirect_dma_start(
                    out=out[:, :], out_offset=bass.IndirectOffsetOnAxis(ap=scatter_idx[:, j:j + 1], axis=0),
                    in_=y_w[:, j % 2, :], in_offset=None, compute_op=ALU.add,
                ).then_inc(scattered, 16)
            pool.wait_ge(scattered, 16 * NT)

        @block.scalar
        def _(act):
            def hi_part(dst, src, done):
                nc.scalar.activation(dst, src, ACT.Copy).then_inc(done, 1)

            for k in range(KC):
                act.wait_ge(x_in[k], 32)
                nc.scalar.activation(w1_hi[:, k, :], w1_raw[:, k, :], ACT.Copy)
                hi_part(x_hi[:, k, :], x_raw[:, k, :], x_hi_ok)
            act.wait_ge(small_in, 80)
            hi_part(w2_hi[:, :, :], w2_raw[:, :, :], wsm_hi_ok)
            act.wait_ge(mid_in, 80)
            hi_part(bw_st[:, :, 0:S], bw_raw[:, :, :], wsm_hi_ok)
            hi_part(gw_hi[:, :, :], gw_raw[:, :, :], wsm_hi_ok)
            hi_part(cw_hi[:, :], cw_raw[:, :], wsm_hi_ok)
            hi_part(rw1_hi[:, :, :], rw1_raw[:, :, :], wsm_hi_ok)
            for k in range(2):
                for oc in range(DC):
                    act.wait_ge(embed_done, k * DC + oc + 1)
                    b = bank[k * DC + oc]
                    nc.scalar.activation(h1_raw[:, oc, half(k)], b[:, :], ACT.Silu, bias=vec[:, V_B1 + oc:V_B1 + oc + 1])
                    nc.scalar.activation(h1_hi[:, oc, half(k)], b[:, :], ACT.Silu,
                                         bias=vec[:, V_B1 + oc:V_B1 + oc + 1]).then_inc(silu_done, 1)
            nc.scalar.activation(decay[:, :], vec[:, V_LD:V_LD + DC], ACT.Sigmoid).then_inc(decay_ok, 1)

            def w1e_high(e):
                act.wait_ge(w1e_in[e], 16)
                hi_part(w1e_hi[:, e], w1e_raw[:, e], w1e_hi_ok)

            w1e_high(0)
            w1e_high(1)
            for k in range(2):
                for c in range(DC):
                    act.wait_ge(xnT_done, k * DC + c + 1)
                    hi_part(xT_hi[:, c, half(k)], bank[k * DC + c][:, :], xT_hi_ok)
            for k in range(2):
                act.wait_ge(bu_done, k + 1)
                hi_part(bu_hi[:, half(k)], bank[4 + k][:, :], bu_hi_ok)
                for oc in range(DC):
                    act.wait_ge(gate_done, k * DC + oc + 1)
                    nc.scalar.activation(gate[:, oc, half(k)], bank[6 + oc][:, :], ACT.Sigmoid,
                                         bias=vec[:, V_GB + oc:V_GB + oc + 1]).then_inc(gate_ok, 1)
            w1e_high(2)
            w1e_high(3)
            for k in range(2):
                for c in range(DC):
                    act.wait_ge(xnT_done, 4 + k * DC + c + 1)
                    hi_part(xT_hi[:, c, half(k)], bank[k * DC + c][:, :], xT_hi_ok)
            act.wait_ge(attnT_done, G)
            for n in range(2 * RC):
                k, rc = divmod(n, RC)
                act.wait_ge(router_done, n + 1)
                nc.scalar.activation(rh[:, rc, half(k)], bank[4 + n % 4][:, :], ACT.Gelu,
                                     bias=vec[:, V_RB1 + rc:V_RB1 + rc + 1]).then_inc(rh_ok, 1)
            act.wait_ge(shifted_ok, 1)
            nc.scalar.activation(ex[:, :, :], lg[:, :, :], ACT.Exp).then_inc(exp_ok, 1)
            act.wait_ge(logits_done, 2)
            for e in range(E):
                act.wait_ge(w2e_in[e], 16)
                hi_part(w2e_hi[:, e], w2e_raw[:, e], w2e_hi_ok)

            def xg_high(j, par):
                act.wait_ge(xgT_done, j + 1)
                hi_part(xg_hi[:, par], bank[3][:, 0:D].rearrange("p (c t) -> p c t", c=DC), xg_hi_ok)

            def gelu(j, par, first):
                for n in range(2):
                    act.wait_ge(hT_done, 2 * j + n + 1)
                    if not first and n == 0:
                        act.wait_ge(down_done, j - 1)
                    src = bank[6 + n][:, :].rearrange("p (c t) -> p c t", t=P)
                    nc.scalar.activation(hT_raw[:, par, 4 * n:4 * n + 4], src, ACT.Gelu)
                    nc.scalar.activation(hT_hi[:, par, 4 * n:4 * n + 4], src, ACT.Gelu).then_inc(gelu_ok, 1)

            def weigh(j, par, first):
                act.wait_ge(y_ok, j + 1)
                if not first:
                    act.wait_ge(scattered, 16 * (j - 1))
                nc.scalar.activation(y_w[:, par, :], y[:, par, :], ACT.Copy,
                                     scale=slot_w[:, bass.ds(j, 1)]).then_inc(yw_ok, 1)

            def step(i, par, lo=True):
                if lo or i + 1 < NT:
                    xg_high(i + 1, 1 - par)
                gelu(i - 1, 1 - par, False)
                weigh(i - 2, par, False)

            xg_high(0, 0)
            xg_high(1, 1)
            xg_high(2, 0)
            gelu(0, 0, True)
            xg_high(3, 1)
            gelu(1, 1, True)
            weigh(0, 0, True)
            xg_high(4, 0)
            gelu(2, 0, False)
            weigh(1, 1, True)
            with act.Fori(FULL.start, FULL.stop, 2) as i:
                step(i, 0)
                step(i + 1, 1)
            for i in range(FULL.stop, NT + 2):
                if i - 1 < NT:
                    gelu(i - 1, (i - 1) % 2, False)
                weigh(i - 2, i % 2, False)

        @block.vector
        def _(dve):
            steps = [0]
            V = nc.vector

            def then(ins):
                steps[0] += 1
                ins.then_inc(dve_step, 1)
                dve.wait_ge(dve_step, steps[0])

            def lo_part(dst, src, hi, done):
                V.tensor_tensor(dst, src, bf(hi), ALU.subtract).then_inc(done, 1)

            for k in range(KC):
                dve.wait_ge(x_hi_ok, k + 1)
                V.tensor_tensor(w1_lo[:, k, :], w1_raw[:, k, :], bf(w1_hi[:, k, :]), ALU.subtract)
                lo_part(x_lo[:, k, :], x_raw[:, k, :], x_hi[:, k, :], x_ok)
            dve.wait_ge(wsm_hi_ok, 1)
            lo_part(w2_lo[:, :, :], w2_raw[:, :, :], w2_hi[:, :, :], wsm_ok)
            for k in range(2):
                for oc in range(DC):
                    dve.wait_ge(silu_done, k * DC + oc + 1)
                    lo_part(h1_lo[:, oc, half(k)], h1_raw[:, oc, half(k)], h1_hi[:, oc, half(k)], h1_ok)
            dve.wait_ge(wsm_hi_ok, 5)
            lo_part(bw_st[:, :, S:2 * S], bw_raw[:, :, :], bw_st[:, :, 0:S], wsm_ok)
            lo_part(gw_lo[:, :, :], gw_raw[:, :, :], gw_hi[:, :, :], wsm_ok)
            lo_part(cw_lo[:, :], cw_raw[:, :], cw_hi[:, :], wsm_ok)

            def normalise(n):
                k = n % 2
                gs = range(4 * k, 4 * k + 4)
                for g in gs:
                    last = V.bn_stats(stats[:, g, :], h[:, g, :])
                then(last)
                for g in gs:
                    last = V.bn_aggr(mv[:, g, :], stats[:, g, :])
                then(last)
                V.tensor_scalar(veps[:, 4 * k:4 * k + 4], mv[:, 4 * k:4 * k + 4, 1], EPS, None,
                                ALU.add).then_inc(veps_ok, 1)
                dve.wait_ge(rstd_ok, n + 1)
                for g in gs:
                    V.tensor_scalar(xn[:, g, :], h[:, g, :], mv[:, g, 0:1], rstd[:, g:g + 1], ALU.subtract,
                                    ALU.mult).then_inc(xn_ok, 1)

            def xT_low(n):
                k = n % 2
                for c in range(DC):
                    dve.wait_ge(xT_hi_ok, n * DC + c + 1)
                    lo_part(xT_lo[:, c, half(k)], bank[k * DC + c][:, :], xT_hi[:, c, half(k)], xT_ok)

            for k in range(2):
                for g in range(4 * k, 4 * k + 4):
                    dve.wait_ge(tok_done, g + 1)
                    ins = V.tensor_tensor(h[:, g, :], bank[4 + g % 4][:, 0:D], b2_bc[:, :], ALU.add)
                    ins.then_inc(h_ok, 1)
                dve.wait_ge(h_ok, 4 * (k + 1))
                normalise(k)
            for k in range(2):
                xT_low(k)
            then(V.memset(carry[:, :], 1.0))
            V.memset(carry[:, :].rearrange("p (b t) -> p b t", t=SEQ)[:, :, 0:1], 0.0)
            then(V.memset(powers[:, :, :], 1.0))
            dve.wait_ge(decay_ok, 1)
            for c in range(DC):
                last = V.tensor_tensor_scan(powers[:, c, 1:SEQ], decay[:, c:c + 1].broadcast_to([P, SEQ - 1]),
                                            carry[:, 0:1].broadcast_to([P, SEQ - 1]), 1.0, ALU.mult, ALU.add)
            then(last)
            for k in range(2):
                dve.wait_ge(bu_hi_ok, k + 1)
                lo_part(bu_lo[:, half(k)], bank[4 + k][:, :], bu_hi[:, half(k)], bu_ok)
                for oc in range(DC):
                    n = k * DC + oc
                    dve.wait_ge(c_done, n + 1)
                    gv = gate[:, oc, half(k)].rearrange("p (b t) -> p b t", t=SEQ)
                    sv = scan_out[:, oc, half(k)].rearrange("p (b t) -> p b t", t=SEQ)
                    then(V.tensor_tensor(sv, bank[n][:, :].rearrange("p (b t) -> p b t", t=SEQ),
                                         powers[:, oc, :].unsqueeze(1).broadcast_to([P, HT // SEQ, SEQ]), ALU.mult))
                    then(V.tensor_tensor_scan(scan_out[:, oc, half(k)], carry[:, :], scan_out[:, oc, half(k)], 0.0,
                                              ALU.mult, ALU.add))
                    dve.wait_ge(gate_ok, n + 1)
                    V.tensor_tensor(gv[:, :, 1:SEQ], gv[:, :, 1:SEQ], sv[:, :, 0:SEQ - 1], ALU.mult)
                    V.memset(gv[:, :, 0:1], 0.0).then_inc(attn_ok, 1)
            lo_part(rw1_lo[:, :, :], rw1_raw[:, :, :], rw1_hi[:, :, :], wsm_ok)
            for k in range(2):
                for g in range(4 * k, 4 * k + 4):
                    dve.wait_ge(attnT_done, g + 1)
                    V.tensor_tensor(h[:, g, :], bank[4 + g % 4][:, 0:D], h[:, g, :], ALU.add).then_inc(h2_ok, 1)
                dve.wait_ge(h2_ok, 4 * (k + 1))
                normalise(2 + k)
            for k in range(2):
                xT_low(2 + k)

            def up(ap, n):
                return ap.unsqueeze(2).broadcast_to([P, ap.shape[1], n])

            def lead(ap, n):
                return ap.unsqueeze(1).broadcast_to([P, n, ap.shape[1]])

            def ge(ap):
                return ap.rearrange("p e g -> p g e")

            dve.wait_ge(logits_done, 2)
            then(V.tensor_tensor(lg[:, :, :], bank[0][:, 0:G * E].rearrange("p (g e) -> p g e", e=E),
                                 lead(rb2_bc[:, :], G), ALU.add))
            then(V.tensor_reduce(lmax[:, :], lg[:, :, :], AX.X, ALU.max))
            V.tensor_tensor(lg[:, :, :], lg[:, :, :], up(lmax[:, :], E), ALU.subtract).then_inc(shifted_ok, 1)
            dve.wait_ge(exp_ok, 1)
            then(V.tensor_reduce(lsum[:, :], ex[:, :, :], AX.X, ALU.add))
            then(V.reciprocal(lrec[:, :], lsum[:, :]))
            then(V.tensor_tensor(pr[:, :, :], ex[:, :, :], up(lrec[:, :], E), ALU.mult))
            pj = pr[:, :, :].unsqueeze(2).broadcast_to([P, G, E, E])
            pe_ = pr[:, :, :].unsqueeze(3).broadcast_to([P, G, E, E])
            V.tensor_tensor(beats[:, :, :, :], pj, pe_, ALU.is_gt)
            then(V.tensor_tensor(ties[:, :, :, :], pj, pe_, ALU.is_equal))
            t4 = ties[:, :, :, :].rearrange("p g e j -> p g (e j)")
            b4 = beats[:, :, :, :].rearrange("p g e j -> p g (e j)")
            then(V.tensor_tensor(t4, t4, lead(cst[:, C_TRI4:C_TRI4 + E * E], G), ALU.mult))
            then(V.tensor_tensor(b4, b4, t4, ALU.add))
            then(V.tensor_reduce(rank[:, :, :], beats[:, :, :, :], AX.X, ALU.add))
            V.tensor_scalar(ge(mask[:, :, :]), rank[:, :, :], TOPK - 0.5, None, ALU.is_lt).then_inc(mask_ok, 1)
            dve.wait_ge(counts_done, 1)
            below = bank[1][:, 0:E * G].rearrange("p (e g) -> p e g", g=G)
            whole = bank[1][:, E * G:2 * E * G]
            flat = lambda t: t[:, :, :].rearrange("p e g -> p (e g)")
            then(V.tensor_tensor_scan(flat(incl), cst[:, C_RESET:C_RESET + E * G], whole, 0.0, ALU.mult, ALU.add))
            then(V.tensor_tensor(full[:, :, :], incl[:, :, G - 1:G].broadcast_to([P, E, G]),
                                 lead(cst[:, C_THR8:C_THR8 + G], E), ALU.is_gt))
            then(V.tensor_reduce(ntile[:, :], full[:, :, :], AX.X, ALU.add))
            then(V.tensor_tensor_scan(tincl[:, :], cst[:, C_ONES:C_ONES + E], ntile[:, :], 0.0, ALU.mult, ALU.add))
            then(V.tensor_tensor(tstart[:, :], tincl[:, :], ntile[:, :], ALU.subtract))
            then(V.tensor_tensor(reach[:, :, :], up(cst[:, C_IOTA20:C_IOTA20 + NTP], E - 1),
                                 lead(tstart[:, 1:E], NTP), ALU.is_ge))
            then(V.tensor_reduce(e_f[:, :], reach[:, :, :], AX.X, ALU.add))
            V.tensor_copy(e_of_tile[:, :], e_f[:, :]).then_inc(emap_ok, 1)
            then(V.tensor_tensor(flat(incl), flat(incl), whole, ALU.subtract))
            then(V.tensor_tensor(incl[:, :, :], incl[:, :, :], below, ALU.add))
            then(V.scalar_tensor_tensor(pos[:, :, :], up(tstart[:, :], G), float(P), incl[:, :, :], ALU.mult, ALU.add))
            then(V.scalar_tensor_tensor(selpos[:, :, :], pos[:, :, :], 1.0, mask[:, :, :], ALU.add, ALU.mult))
            V.tensor_reduce(pos2[:, 1, :], ge(selpos[:, :, :]), AX.X, ALU.max)
            then(V.tensor_reduce(psum2[:, :], ge(selpos[:, :, :]), AX.X, ALU.add))
            V.tensor_tensor(pos2[:, 0, :], psum2[:, :], pos2[:, 1, :], ALU.subtract)
            then(V.tensor_tensor(isb[:, :, :], selpos[:, :, :], lead(pos2[:, 1, :], E), ALU.is_equal))
            then(V.tensor_tensor(isa[:, :, :], mask[:, :, :], isb[:, :, :], ALU.subtract))
            then(V.tensor_tensor(isb[:, :, :], isb[:, :, :], pr[:, :, :].rearrange("p g e -> p e g"), ALU.mult))
            then(V.tensor_tensor(isa[:, :, :], isa[:, :, :], pr[:, :, :].rearrange("p g e -> p e g"), ALU.mult))
            V.tensor_reduce(w2s[:, 0, :], ge(isa[:, :, :]), AX.X, ALU.add)
            then(V.tensor_reduce(w2s[:, 1, :], ge(isb[:, :, :]), AX.X, ALU.add))
            w2f = w2s[:, :, :].rearrange("p a g -> p (a g)")
            p2f = pos2[:, :, :].rearrange("p a g -> p (a g)")
            s2f = slot2[:, :, :].rearrange("p a g -> p (a g)")
            then(V.tensor_scalar(s2f, p2f, -1.0, None, ALU.add))
            then(V.tensor_tensor(thr_ge[:, :, :], up(s2f, NT), lead(cst[:, C_THR19:C_THR19 + NT], 2 * G), ALU.is_ge))
            then(V.tensor_reduce(hi2[:, :], thr_ge[:, :, :], AX.X, ALU.add))
            V.scalar_tensor_tensor(lo2[:, :], hi2[:, :], -float(P), s2f, ALU.mult, ALU.add)
            then(V.tensor_tensor(oh_hi[:, :, :], up(hi2[:, :], NTP), lead(cst[:, C_IOTA20:C_IOTA20 + NTP], 2 * G),
                                 ALU.is_equal))
            for a in range(2):
                V.tensor_copy(vals[:, a * G:(a + 1) * G, 0], cst[:, C_TOK1:C_TOK1 + G])
            then(V.tensor_copy(vals[:, :, 1].bitcast(f32r), w2f))
            then(V.tensor_tensor(vals[:, :, 2], w2f, vals[:, :, 1], ALU.subtract))
            V.tensor_tensor(tab_rhs[:, :, :, :], oh_hi[:, :, :].unsqueeze(2).broadcast_to([P, 2 * G, 3, NTP]),
                            vals[:, :, :].unsqueeze(3).broadcast_to([P, 2 * G, 3, NTP]), ALU.mult)
            V.tensor_tensor(oh_lo[:, :, :], lead(cst[:, C_IOTA:C_IOTA + P], 2 * G), up(lo2[:, :], P),
                            ALU.is_equal).then_inc(onehot_ok, 1)
            dve.wait_ge(table_done, 1)
            then(V.tensor_copy(tab[:, :, :], bank[2][:, 0:3 * NTP].rearrange("p (k j) -> p k j", k=3)))
            V.tensor_tensor(slot_w[:, :], tab[:, 1, :], tab[:, 2, :], ALU.add)
            V.tensor_scalar(gather_idx[:, :], tab[:, 0, :], -1.0, 0.0, ALU.add, ALU.max)
            then(V.tensor_scalar(padz[:, :], tab[:, 0, :], 0.0, cst[:, C_PAD:C_PAD + 1], ALU.is_equal, ALU.mult))
            V.scalar_tensor_tensor(scatter_idx[:, :], tab[:, 0, :], -1.0, padz[:, :], ALU.add,
                                   ALU.add).then_inc(idx_ok, 1)
            for e in range(E):
                dve.wait_ge(w2e_hi_ok, e + 1)
                lo_part(w2e_lo[:, e], w2e_raw[:, e], w2e_hi[:, e], w2e_ok)
            dve.wait_ge(be_in, 32)
            dve.wait_ge(emap_ok, 1)

            def evacuate(i, par, first):
                e = dve.value_load(e_of_tile[0:1, bass.ds(i, 1)], min_val=0, max_val=E - 1)
                for n in range(2):
                    dve.wait_ge(up_done, 2 * i + n + 1)
                    if not first:
                        dve.wait_ge(hT_done, 2 * i - 3 + n)
                    V.tensor_tensor(hpre[:, par, n * 512:(n + 1) * 512], bank[4 + n][:, :],
                                    be1_bc[:, bass.ds(e, 1), n * 512:(n + 1) * 512].squeeze(1), ALU.add).then_inc(hpre_ok, 1)

            def xg_low(j, par):
                dve.wait_ge(xg_hi_ok, j + 1)
                lo_part(xg_lo[:, par], bank[3][:, 0:D].rearrange("p (c t) -> p c t", c=DC), xg_hi[:, par], xg_ok)

            def split(j, par):
                for n in range(2):
                    dve.wait_ge(gelu_ok, 2 * j + n + 1)
                    s = slice(4 * n, 4 * n + 4)
                    lo_part(hT_lo[:, par, s], hT_raw[:, par, s], hT_hi[:, par, s], hT_ok)

            def result(j, par, first):
                e = dve.value_load(e_of_tile[0:1, bass.ds(j, 1)], min_val=0, max_val=E - 1)
                dve.wait_ge(down_done, j + 1)
                if not first:
                    dve.wait_ge(yw_ok, j - 1)
                V.tensor_tensor(y[:, par, :], bank[par][:, 0:D],
                                be2_bc[:, bass.ds(e, 1), :].squeeze(1), ALU.add).then_inc(y_ok, 1)

            def step(i, par):
                evacuate(i, par, False)
                xg_low(i + 1, 1 - par)
                split(i - 1, 1 - par)
                result(i - 2, par, False)

            xg_low(0, 0)
            for i in range(4):
                evacuate(i, i % 2, i < 2)
                xg_low(i + 1, (i + 1) % 2)
                if i >= 1:
                    split(i - 1, (i - 1) % 2)
                if i >= 2:
                    result(i - 2, i % 2, i - 2 < 2)
            with dve.Fori(FULL.start, FULL.stop, 2) as i:
                step(i, 0)
                step(i + 1, 1)
            for i in range(FULL.stop, NT + 2):
                if i < NT:
                    evacuate(i, i % 2, False)
                if i - 1 < NT:
                    split(i - 1, (i - 1) % 2)
                result(i - 2, i % 2, False)

        @block.tensor
        def _(pe):
            T = nc.tensor

            def three(dst, st_hi, st_lo, mv_hi, mv_lo, first, last):
                T.matmul(dst, st_hi, mv_hi, start=first, stop=False)
                T.matmul(dst, st_hi, mv_lo, start=False, stop=False)
                return T.matmul(dst, st_lo, mv_hi, start=False, stop=last)

            for k in range(KC):
                pe.wait_ge(x_ok, k + 1)
                for hf in range(2):
                    for oc in range(DC):
                        o = slice(oc * P, (oc + 1) * P)
                        ins = three(bank[hf * DC + oc][:, :], w1_hi[:, k, o], w1_lo[:, k, o],
                                    x_hi[:, k, half(hf)], x_lo[:, k, half(hf)], k == 0, k == KC - 1)
                        if k == KC - 1:
                            ins.then_inc(embed_done, 1)
            pe.wait_ge(wsm_ok, 1)
            for g in range(G):
                pe.wait_ge(h1_ok, DC * (g // 4 + 1))
                if g >= 4:
                    pe.wait_ge(h_ok, g - 3)
                for c in range(DC):
                    ins = three(bank[4 + g % 4][:, 0:D], h1_hi[:, c, rows(g)], h1_lo[:, c, rows(g)],
                                w2_hi[:, c, :], w2_lo[:, c, :], c == 0, c == DC - 1)
                ins.then_inc(tok_done, 1)

            def transpose_xn(n):
                k = n % 2
                for c in range(DC):
                    for g in range(4 * k, 4 * k + 4):
                        pe.wait_ge(xn_ok, (n // 2) * G + g + 1)
                        ins = T.transpose(bank[k * DC + c][:, rows(g % 4)], xn[:, g, c * P:(c + 1) * P], ident)
                    ins.then_inc(xnT_done, 1)

            transpose_xn(0)
            transpose_xn(1)
            pe.wait_ge(wsm_ok, 4)
            for k in range(2):
                pe.wait_ge(xT_ok, DC * (k + 1))
                pe.wait_ge(h_ok, G)
                dst = bank[4 + k][:, :]
                for c in range(DC):
                    T.matmul(dst, bw_st[:, c, :], xT_hi[:, c, half(k)], start=c == 0, stop=False)
                    ins = T.matmul(dst, bw_st[:, c, :], xT_lo[:, c, half(k)], start=False, stop=c == DC - 1)
                ins.then_inc(bu_done, 1)
                for oc in range(DC):
                    o = slice(oc * P, (oc + 1) * P)
                    if k == 1:
                        pe.wait_ge(gate_ok, oc + 1)
                    for c in range(DC):
                        ins = three(bank[6 + oc][:, :], gw_hi[:, c, o], gw_lo[:, c, o],
                                    xT_hi[:, c, half(k)], xT_lo[:, c, half(k)], c == 0, c == DC - 1)
                    ins.then_inc(gate_done, 1)
                pe.wait_ge(bu_ok, k + 1)
                for oc in range(DC):
                    o = slice(oc * P, (oc + 1) * P)
                    three(bank[k * DC + oc][:, :], cw_hi[:, o], cw_lo[:, o], bu_hi[:, half(k)], bu_lo[:, half(k)],
                          True, True).then_inc(c_done, 1)
            pe.wait_ge(gate_ok, 2 * DC)
            for g in range(G):
                pe.wait_ge(attn_ok, DC * (g // 4 + 1))
                if g >= 4:
                    pe.wait_ge(h2_ok, g - 3)
                for c in range(DC):
                    ins = T.transpose(bank[4 + g % 4][:, c * P:(c + 1) * P], gate[:, c, rows(g)], ident)
                ins.then_inc(attnT_done, 1)
            transpose_xn(2)
            transpose_xn(3)
            pe.wait_ge(wsm_ok, 5)
            for n in range(2 * RC):
                k, rc = divmod(n, RC)
                pe.wait_ge(xT_ok, 2 * DC + DC * (k + 1))
                pe.wait_ge(h2_ok, G)
                if n >= 4:
                    pe.wait_ge(rh_ok, n - 3)
                o = slice(rc * P, (rc + 1) * P)
                for c in range(DC):
                    ins = three(bank[4 + n % 4][:, :], rw1_hi[:, c, o], rw1_lo[:, c, o],
                                xT_hi[:, c, half(k)], xT_lo[:, c, half(k)], c == 0, c == DC - 1)
                ins.then_inc(router_done, 1)
            for g in range(G):
                pe.wait_ge(rh_ok, RC * (g // 4 + 1))
                for rc in range(RC):
                    ins = T.matmul(bank[0][:, g * E:(g + 1) * E], rh[:, rc, rows(g)],
                                   vec[:, V_RW2 + rc * E:V_RW2 + (rc + 1) * E], start=rc == 0, stop=rc == RC - 1)
                if g % 4 == 3:
                    ins.then_inc(logits_done, 1)
            pe.wait_ge(mask_ok, 1)
            mflat = mask[:, :, :].rearrange("p e g -> p (e g)")
            T.matmul(bank[1][:, 0:E * G], cst[:, C_TRI:C_TRI + P], mflat, start=True, stop=True)
            T.matmul(bank[1][:, E * G:2 * E * G], cst[:, C_ONES:C_ONES + P], mflat, start=True,
                     stop=True).then_inc(counts_done, 1)
            pe.wait_ge(onehot_ok, 1)
            for a in range(2 * G):
                ins = T.matmul(bank[2][:, 0:3 * NTP], oh_lo[:, a, :],
                               tab_rhs[:, a].rearrange("p k j -> p (k j)"), start=a == 0, stop=a == 2 * G - 1)
            ins.then_inc(table_done, 1)

            def turn_in(j, par, count):
                pe.wait_ge(gathered[par], 16 * count)
                if not isinstance(j, int) or j >= 1:
                    pe.wait_ge(xg_ok, j)
                for c in range(DC):
                    ins = T.transpose(bank[3][:, c * P:(c + 1) * P], xg[:, par, c * P:(c + 1) * P], ident)
                ins.then_inc(xgT_done, 1)

            def up_proj(i, par, first):
                e = pe.value_load(e_of_tile[0:1, bass.ds(i, 1)], min_val=0, max_val=E - 1)
                pe.wait_ge(xg_ok, i + 1)
                for n in range(2):
                    if not first:
                        pe.wait_ge(hpre_ok, 2 * i - 1 + n)
                    hs = slice(n * 512, (n + 1) * 512)
                    for c in range(DC):
                        w_hi = w1e_hi[:, bass.ds(e, 1), c, hs].squeeze(1)
                        w_lo = w1e_lo[:, bass.ds(e, 1), c, hs].squeeze(1)
                        ins = three(bank[4 + n][:, :], xg_hi[:, par, c, :], xg_lo[:, par, c, :], w_hi, w_lo,
                                    c == 0, c == DC - 1)
                    ins.then_inc(up_done, 1)

            def turn(j, par, first):
                for n in range(2):
                    pe.wait_ge(hpre_ok, 2 * j + n + 1)
                    if not first:
                        pe.wait_ge(gelu_ok, 2 * j - 1 + n)
                    for c in range(4):
                        hc = 4 * n + c
                        ins = T.transpose(bank[6 + n][:, rows(c)], hpre[:, par, hc * P:(hc + 1) * P], ident)
                    ins.then_inc(hT_done, 1)

            def down_proj(j, par, first):
                e = pe.value_load(e_of_tile[0:1, bass.ds(j, 1)], min_val=0, max_val=E - 1)
                if not first:
                    pe.wait_ge(y_ok, j - 1)
                for hc in range(HC):
                    if hc % 4 == 0:
                        pe.wait_ge(hT_ok, 2 * j + hc // 4 + 1)
                    w_hi = w2e_hi[:, bass.ds(e, 1), hc, :].squeeze(1)
                    w_lo = w2e_lo[:, bass.ds(e, 1), hc, :].squeeze(1)
                    ins = three(bank[par][:, 0:D], hT_hi[:, par, hc, :], hT_lo[:, par, hc, :], w_hi, w_lo,
                                hc == 0, hc == HC - 1)
                ins.then_inc(down_done, 1)

            pe.wait_ge(emap_ok, 1)
            turn_in(0, 0, 1)
            pe.wait_ge(w1e_ok, E)
            for i in range(4):
                up_proj(i, i % 2, i == 0)
                turn_in(i + 1, (i + 1) % 2, (i + 1) // 2 + 1)
                if i >= 1:
                    turn(i - 1, (i - 1) % 2, i - 1 == 0)
                if i == 2:
                    pe.wait_ge(w2e_ok, E)
                if i >= 2:
                    down_proj(i - 2, i % 2, i - 2 < 2)
            with pe.Fori(FULL.start // 2, FULL.stop // 2) as m:
                for par in range(2):
                    i = 2 * m + par
                    up_proj(i, par, False)
                    turn_in(i + 1, 1 - par, m + 1 + par)
                    turn(i - 1, 1 - par, False)
                    down_proj(i - 2, par, False)
            for i in range(FULL.stop, NT + 2):
                if i < NT:
                    up_proj(i, i % 2, False)
                if i - 1 < NT:
                    turn(i - 1, (i - 1) % 2, False)
                down_proj(i - 2, i % 2, False)


def kernel(**inputs):
    import numpy as np
    import concourse.bacc as bacc
    from concourse import mybir as mb
    from concourse.bass_utils import run_bass_kernel_spmd

    a = {k.replace("L0_", ""): np.asarray(v) for k, v in inputs.items()}
    gh = 4
    xT = a["x"].reshape(64, 3, gh, 16, gh, 16).transpose(1, 3, 5, 0, 2, 4).reshape(KC, P, TOKENS)

    def cols(v):
        return v.reshape(-1, P).T

    vecs = np.concatenate([cols(a["tok_b1"]), cols(a["attn_gate_b"]), cols(a["attn_log_decay"]), cols(a["ffn_rb1"]),
                           a["ffn_rW2"].reshape(RC, P, E).transpose(1, 0, 2).reshape(P, RC * E)], axis=1)
    p = np.arange(P)
    one = np.ones((P, 1))
    consts = np.concatenate([
        np.eye(P), one * p, p[:, None] < p[None, :], np.ones((P, P)), one * (P * np.arange(1, NT + 1)),
        one * np.arange(NTP), one * (P * np.arange(G)), p[:, None] + P * np.arange(G) + 1, p[:, None] + TOKENS + 1,
        one * (np.arange(E)[None, :] < np.arange(E)[:, None]).reshape(1, -1),
        one * (np.arange(E * G) % G != 0), np.full((P, G), -0.5)], axis=1).astype(np.float32)
    arrays = {
        "xT": xT, "w1": a["tok_W1"], "w2": a["tok_W2"], "b2": a["tok_b2"], "bw": a["attn_B_w"].T, "cw": a["attn_C_w"].T,
        "gw": a["attn_gate_w"].T, "rw1": a["ffn_rW1"], "rb2": a["ffn_rb2"], "we1": a["ffn_We1"], "be1": a["ffn_be1"],
        "we2": a["ffn_We2"], "be2": a["ffn_be2"], "vecs": vecs, "consts": consts,
    }
    arrays = {k: np.ascontiguousarray(v) for k, v in arrays.items()}
    nc = bacc.Bacc("TRN2", target_bir_lowering=False, num_devices=1)
    aps = {k: nc.dram_tensor(f"in_{k}", v.shape, mb.dt.from_np(v.dtype), kind="ExternalInput").ap()
           for k, v in arrays.items()}
    out = nc.dram_tensor("out_rows", (TOKENS + P, D), mb.dt.float32, kind="ExternalOutput").ap()
    tower(nc, *(aps[k] for k in arrays), out)
    r = run_bass_kernel_spmd(nc, [{f"in_{k}": v for k, v in arrays.items()}], core_ids=[0])
    return r.results[0]["out_rows"][:TOKENS].reshape(64, SEQ, D)
```

```python
import concourse.bass as bass
from concourse import mybir

TOKENS, D, KP, S, R, E, HID = 1024, 256, 768, 64, 512, 4, 1024
SEQ = 16
P = 128
G = TOKENS // P
HT = TOKENS // 2
DC, KC, RC, HC = D // P, KP // P, R // P, HID // P
TOPK = 2
NT = (TOPK * TOKENS + E * (P - 1)) // P
TILE_BITS = P.bit_length() - 1
NTP = NT + 1
EPS = 1e-5

C_IDENT, C_IOTA, C_TRI, C_ONES = 0, 128, 256, 384
C_IOTA20 = 512
C_THR8 = C_IOTA20 + NTP
C_TOK1 = C_THR8 + G
C_PAD = C_TOK1 + G
C_ORDER = C_PAD + 1
C_RESET = C_ORDER + E * 2 * E
C_NEGHALF = C_RESET + E * G
C_COLS = C_NEGHALF + G
V_B1, V_GB, V_LD, V_RB1, V_RW2 = 0, DC, 2 * DC, 3 * DC, 3 * DC + RC
V_COLS = V_RW2 + RC * E


def tower(nc, xT, w1, w2, b2, bw, cw, gw, rw1, rb2, we1, be1, we2, be2, vecs, consts, out):
    f32, f32r, i32 = mybir.dt.float32, mybir.dt.float32r, mybir.dt.int32
    ALU = mybir.AluOpType
    ACT = mybir.ActivationFunctionType
    AX = mybir.AxisListType

    BASE = 16512
    KB = 1024

    def place(name, shape, at, dt=f32):
        return nc.alloc_sbuf_tensor_at(name, [P] + shape, dt, offset=BASE + int(at * KB))

    w1e_hi = place("w1e_hi", [E, DC, HID], 0, f32r)
    w1e_raw = place("w1e_raw", [E, DC, HID], 32)
    w1e_lo = place("w1e_lo", [E, DC, HID], 32, f32r)
    w2e_hi = place("w2e_hi", [E, HC, D], 64, f32r)
    w2e_raw = place("w2e_raw", [E, HC, D], 96)
    w2e_lo = place("w2e_lo", [E, HC, D], 96, f32r)
    x_hi = place("x_hi", [KC, TOKENS], 64, f32r)
    w1_hi = place("w1_hi", [KC, D], 88, f32r)
    x_raw = place("x_raw", [KC, TOKENS], 96)
    x_lo = place("x_lo", [KC, TOKENS], 96, f32r)
    w1_raw = place("w1_raw", [KC, D], 120)
    w1_lo = place("w1_lo", [KC, D], 120, f32r)
    bu_hi = place("bu_hi", [TOKENS], 72, f32r)
    bu_lo = place("bu_lo", [TOKENS], 76, f32r)
    scan_out = place("scan_out", [DC, TOKENS], 80)
    gate = place("gate", [DC, TOKENS], 88)
    carry = place("carry", [HT], 142)
    powers = place("powers", [DC, SEQ], 207.25)
    rh_hi = place("rh_hi", [4, HT], 128, f32r)
    rh_raw = place("rh_raw", [4, HT], 136)
    rh_lo = place("rh_lo", [4, HT], 136, f32r)
    rw2_st = place("rw2_st", [RC, P], 203.75, f32r)
    logitsT = place("logitsT", [TOKENS], 164.75)
    be1_bc = place("be1_bc", [E, HID], 128)
    be2_bc = place("be2_bc", [E, D], 144)
    b2_bc = place("b2_bc", [D], 148)
    cst = place("cst", [C_COLS], 149)
    vec = place("vec", [V_COLS], 151.75)
    rb2_bc = place("rb2_bc", [E], 151.875)
    decay = place("decay", [DC], 151.90625)
    stats = place("stats", [G, 6], 151.9375)
    mv = place("mv", [G, 2], 152.125)
    veps = place("veps", [G], 152.1875)
    rstd = place("rstd", [G], 152.21875)
    shift = place("shift", [G], 152.625)
    e_of_tile = place("e_of_tile", [NTP], 152.25, i32)
    gather_idx = place("gather_idx", [NTP], 152.34375, i32)
    scatter_idx = place("scatter_idx", [NTP], 152.4375, i32)
    slot_w = place("slot_w", [NTP], 152.53125)
    rw1_hi = place("rw1_hi", [DC, R], 152.75, f32r)
    rw1_raw = place("rw1_raw", [DC, R], 156.75)
    rw1_lo = place("rw1_lo", [DC, R], 156.75, f32r)
    gw_hi = place("gw_hi", [DC, D], 160.75, f32r)
    gw_raw = place("gw_raw", [DC, D], 162.75)
    gw_lo = place("gw_lo", [DC, D], 162.75, f32r)
    w2_hi = place("w2_hi", [DC, D], 164.75, f32r)
    w2_raw = place("w2_raw", [DC, D], 166.75)
    w2_lo = place("w2_lo", [DC, D], 166.75, f32r)
    cw_hi = place("cw_hi", [D], 168.75, f32r)
    cw_raw = place("cw_raw", [D], 169.75)
    cw_lo = place("cw_lo", [D], 169.75, f32r)
    bw_st = place("bw_st", [DC, 2 * S], 170.75, f32r)
    bw_raw = place("bw_raw", [DC, S], 206.75)
    h = place("h", [G, D], 171.75)
    xn = place("xn", [G, D], 179.75)
    h1_hi = place("h1_hi", [DC, TOKENS], 187.75, f32r)
    h1_raw = place("h1_raw", [DC, TOKENS], 195.75)
    h1_lo = place("h1_lo", [DC, TOKENS], 195.75, f32r)
    xT_hi = place("xT_hi", [DC, TOKENS], 187.75, f32r)
    xT_lo = place("xT_lo", [DC, TOKENS], 195.75, f32r)
    zero = place("zero", [D], 205.75)
    unused = place("unused", [1], 207.5)
    CH = 168.75
    lg = place("lg", [G, E], CH)
    lmax = place("lmax", [G], CH + .125)
    lsum = place("lsum", [G], CH + .15625)
    lrec = place("lrec", [G], CH + .1875)
    ex = place("ex", [G, E], CH + .25)
    pr = place("pr", [G, E], CH + .375)
    beats = place("beats", [G, E, 2, E], CH + .5)
    rank = place("rank", [G, E], CH + 1.5)
    mask = place("mask", [E, G], CH + 1.625)
    incl = place("incl", [E, G], CH + 1.75)
    RT = 152.75
    full = place("full", [E, G], RT + 1.875)
    ntile = place("ntile", [E], RT + 2)
    base = place("base", [E], RT + 2.03125)
    tstart = place("tstart", [E], RT + 2.0625)
    reach = place("reach", [NTP, E - 1], RT + 2.125)
    e_f = place("e_f", [NTP], RT + 2.375)
    selpos = place("selpos", [E, G], RT + 2.625)
    isb = place("isb", [E, G], RT + 2.75)
    isa = place("isa", [E, G], RT + 2.875)
    psum2 = place("psum2", [G], RT + 3)
    pos2 = place("pos2", [2, G], RT + 3.0625)
    w2s = place("w2s", [2, G], RT + 3.1875)
    hi2 = place("hi2", [2 * G], RT + 3.25, i32)
    lo2 = place("lo2", [2 * G], RT + 3.3125, i32)
    vals = place("vals", [2 * G, 3], 207.53125)
    slot_no = place("slot_no", [2 * G], RT + 3.75, i32)
    oh_hi = place("oh_hi", [2 * G, NTP], RT + 5)
    tab_rhs = place("tab_rhs", [2 * G, 3, NTP], RT + 6.25, f32r)
    oh_lo = place("oh_lo", [2 * G, P], 187.75, f32r)
    tab = place("tab", [3, NTP], RT + 10)
    padz = place("padz", [NTP], RT + 10.25)
    y = place("y", [2, D], 171.75)
    y_w = place("y_w", [2, D], 173.75)
    xg_hi = place("xg_hi", [2, DC, P], 175.75, f32r)
    xg_lo = place("xg_lo", [2, DC, P], 177.75, f32r)
    hpre = place("hpre", [2, HID], 179.75)
    hT_hi = place("hT_hi", [2, HC, P], 187.75, f32r)
    hT_raw = place("hT_raw", [2, HC, P], 195.75)
    hT_lo = place("hT_lo", [2, HC, P], 195.75, f32r)
    xg = place("xg", [2, D], 203.75)

    xn_rows = nc.dram_tensor("xn_rows", [TOKENS, D], f32, kind="Internal").ap()

    bank = [nc.alloc_psum_tensor(f"bank{i}", [P, 512], f32) for i in range(8)]

    def sem(name):
        return nc.alloc_semaphore(name)

    x_in = [sem(f"x_in{n}") for n in range(2 * KC)]
    vec_in, w2_in, cst_in, mid_in, be_in = sem("vec_in"), sem("w2_in"), sem("cst_in"), sem("mid_in"), sem("be_in")
    w1e_in = [sem(f"w1e_in{e}") for e in range(E)]
    w2e_in = [sem(f"w2e_in{e}") for e in range(E)]
    x_hi_ok, x_ok = sem("x_hi_ok"), sem("x_ok")
    wsm_hi_ok, wsm_ok = sem("wsm_hi_ok"), sem("wsm_ok")
    w1e_hi_ok, w1e_ok = sem("w1e_hi_ok"), sem("w1e_ok")
    w2e_hi_ok, w2e_ok, w2e_last_ok = sem("w2e_hi_ok"), sem("w2e_ok"), sem("w2e_last_ok")
    embed_done, silu_done, h1_ok = sem("embed_done"), sem("silu_done"), sem("h1_ok")
    tok_done, h_ok = sem("tok_done"), sem("h_ok")
    veps_ok, rstd_ok, shift_ok = sem("veps_ok"), sem("rstd_ok"), sem("shift_ok")
    xn_v_ok, xn_a_ok, rw1_ok = sem("xn_v_ok"), sem("xn_a_ok"), sem("rw1_ok")
    xnT_done, xT_hi_ok, xT_ok = sem("xnT_done"), sem("xT_hi_ok"), sem("xT_ok")
    bu_done, bu_hi_ok, bu_ok = sem("bu_done"), sem("bu_hi_ok"), sem("bu_ok")
    gate_done, gate_ok, decay_ok = sem("gate_done"), sem("gate_ok"), sem("decay_ok")
    c_done, attn_ok, attnT_done, h2_ok = sem("c_done"), sem("attn_ok"), sem("attnT_done"), sem("h2_ok")
    router_done, rh_hi_ok, rh_ok = sem("router_done"), sem("rh_hi_ok"), sem("rh_ok")
    rh_used, logitsT_ok, logits_done, rw2_ok = sem("rh_used"), sem("logitsT_ok"), sem("logits_done"), sem("rw2_ok")
    shifted_ok, exp_ok, mask_ok, counts_done = sem("shifted_ok"), sem("exp_ok"), sem("mask_ok"), sem("counts_done")
    vals_ok, told_ok = sem("vals_ok"), sem("told_ok")
    onehot_ok, table_done, emap_ok, idx_ok = sem("onehot_ok"), sem("table_done"), sem("emap_ok"), sem("idx_ok")
    xn_stored, h2_stored, zero_ok = sem("xn_stored"), sem("h2_stored"), sem("zero_ok")
    gathered = [sem("gathered0"), sem("gathered1")]
    xgT_done, xg_hi_ok, xg_ok = sem("xgT_done"), sem("xg_hi_ok"), sem("xg_ok")
    up_done, hpre_ok, hT_done = sem("up_done"), sem("hpre_ok"), sem("hT_done")
    gelu_ok, hT_ok, down_done = sem("gelu_ok"), sem("hT_ok"), sem("down_done")
    y_ok, yw_ok, scattered = sem("y_ok"), sem("yw_ok"), sem("scattered")
    dve_step = sem("dve_step")

    ident = cst[:, C_IDENT:C_IDENT + P]

    def half(k):
        return slice(k * HT, (k + 1) * HT)

    def rows(g):
        return slice(g * P, (g + 1) * P)

    def bf(ap):
        return ap.bitcast(f32)

    RB = (4, 5, 1)
    FULL = range(4, 18)

    with nc.Block() as block:

        @block.sync
        def _(sp):
            for k in range(KC):
                sp.dma_start(x_raw[:, k, half(0)], xT[k, :, half(0)]).then_inc(x_in[k], 16)
                sp.dma_start(w1_raw[:, k, :], w1[k * P:(k + 1) * P, :]).then_inc(x_in[k], 16)
            sp.dma_start(w2_raw[:, :, :], w2.rearrange("(c p) n -> p c n", p=P)).then_inc(w2_in, 16)
            for k in range(KC):
                sp.dma_start(x_raw[:, k, half(1)], xT[k, :, half(1)]).then_inc(x_in[KC + k], 16)
            sp.dma_start(b2_bc[:, :], b2.partition_broadcast(P)).then_inc(cst_in, 16)
            sp.dma_start(cst[:, :], consts[:, :]).then_inc(cst_in, 16)
            sp.dma_start(bw_raw[:, :, :], bw.rearrange("(c p) n -> p c n", p=P)).then_inc(mid_in, 16)
            sp.dma_start(cw_raw[0:S, :], cw[:, :]).then_inc(mid_in, 16)
            sp.dma_start(cw_raw[S:2 * S, :], cw[:, :]).then_inc(mid_in, 16)
            sp.dma_start(gw_raw[:, :, :], gw.rearrange("(c p) n -> p c n", p=P)).then_inc(mid_in, 16)
            sp.dma_start(rw1_raw[:, :, :], rw1.rearrange("(c p) n -> p c n", p=P)).then_inc(mid_in, 16)
            sp.dma_start(rb2_bc[:, :], rb2.partition_broadcast(P)).then_inc(mid_in, 16)
            for e in range(E):
                sp.dma_start(w1e_raw[:, e], we1[e].rearrange("(c p) n -> p c n", p=P)).then_inc(w1e_in[e], 16)
            sp.dma_start(be2_bc[:, :, :], be2.partition_broadcast(P)).then_inc(be_in, 16)
            sp.wait_ge(embed_done, 2 * DC)
            for e in range(E):
                sp.dma_start(w2e_raw[:, e], we2[e].rearrange("(c p) n -> p c n", p=P)).then_inc(w2e_in[e], 16)
            sp.wait_ge(zero_ok, 1)
            sp.dma_start(out[TOKENS:TOKENS + P, :], zero[:, :]).then_inc(h2_stored, 16)
            for k in range(2):
                gs = slice(4 * k, 4 * k + 4)
                sp.wait_ge(h2_ok, 2 * (k + 1))
                sp.dma_start(out[half(k), :].rearrange("(g p) n -> p g n", p=P), h[:, gs, :]).then_inc(h2_stored, 16)
                sp.wait_ge(xn_v_ok, 4 + 2 * (k + 1))
                sp.wait_ge(xn_a_ok, 4 + 2 * (k + 1))
                sp.dma_start(xn_rows[half(k), :].rearrange("(g p) n -> p g n", p=P), xn[:, gs, :]).then_inc(xn_stored, 16)
            sp.wait_ge(rh_used, 2 * RC)
            sp.dma_start(be1_bc[:, :, :], be1.partition_broadcast(P)).then_inc(be_in, 16)

        @block.gpsimd
        def _(pool):
            def inverse_deviation(n):
                k = n % 2
                pool.wait_ge(veps_ok, n + 1)
                nc.gpsimd.tensor_tensor(rstd[:, 4 * k:4 * k + 4], veps[:, 4 * k:4 * k + 4],
                                        cst[:, C_NEGHALF:C_NEGHALF + 4], ALU.pow).then_inc(rstd_ok, 1)

            def w1e_low(e, c):
                pool.wait_ge(w1e_hi_ok, DC * e + c + 1)
                nc.gpsimd.tensor_tensor(w1e_lo[:, e, c], w1e_raw[:, e, c], bf(w1e_hi[:, e, c]),
                                        ALU.subtract).then_inc(w1e_ok, 1)

            def w2e_low(e, part):
                s = slice(4 * part, 4 * part + 4)
                pool.wait_ge(w2e_hi_ok, 2 * e + part + 1)
                nc.gpsimd.tensor_tensor(w2e_lo[:, e, s], w2e_raw[:, e, s], bf(w2e_hi[:, e, s]),
                                        ALU.subtract).then_inc(w2e_ok, 1)

            pool.wait_ge(cst_in, 32)
            inverse_deviation(0)
            pool.wait_ge(wsm_hi_ok, 6)
            nc.gpsimd.tensor_tensor(rw1_lo[:, :, :], rw1_raw[:, :, :], bf(rw1_hi[:, :, :]), ALU.subtract).then_inc(rw1_ok, 1)
            w1e_low(0, 0)
            inverse_deviation(1)
            w1e_low(0, 1)
            w1e_low(1, 0)
            w1e_low(1, 1)
            w1e_low(2, 0)
            inverse_deviation(2)
            w1e_low(2, 1)
            w1e_low(3, 0)
            inverse_deviation(3)
            w1e_low(3, 1)
            w2e_low(0, 0)
            w2e_low(0, 1)
            w2e_low(1, 0)
            w2e_low(1, 1)
            w2e_low(2, 0)
            pool.wait_ge(vals_ok, 1)
            for h2 in range(2):
                t = slice(h2 * G, (h2 + 1) * G)
                nc.gpsimd.tensor_tensor(tab_rhs[:, t, :, :], oh_hi[:, t, :].unsqueeze(2).broadcast_to([P, G, 3, NTP]),
                                        vals[:, t, :].unsqueeze(3).broadcast_to([P, G, 3, NTP]),
                                        ALU.mult).then_inc(told_ok, 1)

            pool.wait_ge(idx_ok, 1)
            pool.wait_ge(xn_stored, 32)

            def gather(j):
                if j >= NT:
                    return
                if j >= 2:
                    pool.wait_ge(gathered[j % 2], 16 * (j // 2))
                    pool.wait_ge(xgT_done, j - 1)
                nc.gpsimd.indirect_dma_start(
                    out=xg[:, j % 2, :], out_offset=None, in_=xn_rows[:, :],
                    in_offset=bass.IndirectOffsetOnAxis(ap=gather_idx[:, j:j + 1], axis=0),
                ).then_inc(gathered[j % 2], 16)

            gather(0)
            gather(1)
            w2e_low(2, 1)
            for j in range(2, 5):
                gather(j)
            pool.wait_ge(h2_stored, 48)
            pool.wait_ge(idx_ok, 2)
            for j in range(NT):
                gather(j + 5)
                if j >= 1:
                    pool.wait_ge(scattered, 16 * j)
                pool.wait_ge(yw_ok, j + 1)
                nc.gpsimd.indirect_dma_start(
                    out=out[:, :], out_offset=bass.IndirectOffsetOnAxis(ap=scatter_idx[:, j:j + 1], axis=0),
                    in_=y_w[:, j % 2, :], in_offset=None, compute_op=ALU.add,
                ).then_inc(scattered, 16)
            pool.wait_ge(scattered, 16 * NT)

        @block.scalar
        def _(act):
            def hi_part(dst, src, done):
                nc.scalar.activation(dst, src, ACT.Copy).then_inc(done, 1)

            act.dma_start(vec[:, :], vecs[:, :]).then_inc(vec_in, 16)
            def table(fn):
                nc.scalar.activation(unused[:, :], vec[:, 0:1], fn)

            def x_high(hf, k):
                n = hf * KC + k
                act.wait_ge(x_in[n], 32 if hf == 0 else 16)
                if hf == 0:
                    nc.scalar.activation(w1_hi[:, k, :], w1_raw[:, k, :], ACT.Copy)
                hi_part(x_hi[:, k, half(hf)], x_raw[:, k, half(hf)], x_hi_ok)

            def silu(k, oc):
                act.wait_ge(embed_done, k * DC + oc + 1)
                b = bank[k * DC + oc]
                nc.scalar.activation(h1_raw[:, oc, half(k)], b[:, :], ACT.Silu, bias=vec[:, V_B1 + oc:V_B1 + oc + 1])
                nc.scalar.activation(h1_hi[:, oc, half(k)], b[:, :], ACT.Silu,
                                     bias=vec[:, V_B1 + oc:V_B1 + oc + 1]).then_inc(silu_done, 1)

            def w1e_high(e, c):
                act.wait_ge(w1e_in[e], 16)
                hi_part(w1e_hi[:, e, c], w1e_raw[:, e, c], w1e_hi_ok)

            def w2e_high(e, part):
                s = slice(4 * part, 4 * part + 4)
                act.wait_ge(w2e_in[e], 16)
                hi_part(w2e_hi[:, e, s], w2e_raw[:, e, s], w2e_hi_ok)

            def normalise(n):
                act.wait_ge(shift_ok, n + 1)
                for g in range(4 * (n % 2) + 2, 4 * (n % 2) + 4):
                    nc.scalar.activation(xn[:, g, :], h[:, g, :], ACT.Identity, bias=shift[:, g:g + 1],
                                         scale=rstd[:, g:g + 1]).then_inc(xn_a_ok, 1)

            def xT_high(n):
                for c in range(DC):
                    act.wait_ge(xnT_done, n * DC + c + 1)
                    hi_part(xT_hi[:, c, half(n % 2)], bank[(n % 2) * DC + c][:, :], xT_hi_ok)

            def bu_high(k):
                act.wait_ge(bu_done, k + 1)
                hi_part(bu_hi[:, half(k)], bank[2 * k][:, :], bu_hi_ok)

            def gates(k, oc):
                act.wait_ge(gate_done, k * DC + oc + 1)
                nc.scalar.activation(gate[:, oc, half(k)], bank[4 + 2 * k + oc][:, :], ACT.Sigmoid,
                                     bias=vec[:, V_GB + oc:V_GB + oc + 1]).then_inc(gate_ok, 1)

            def router(n):
                rc = n % RC
                act.wait_ge(router_done, n + 1)
                if n >= 4:
                    act.wait_ge(rh_used, n - 3)
                for dst in (rh_raw, rh_hi):
                    ins = nc.scalar.activation(dst[:, n % 4, :], bank[RB[n % 3]][:, :], ACT.Gelu,
                                               bias=vec[:, V_RB1 + rc:V_RB1 + rc + 1])
                ins.then_inc(rh_hi_ok, 1)

            act.wait_ge(vec_in, 16)
            nc.scalar.activation(decay[:, :], vec[:, V_LD:V_LD + DC], ACT.Sigmoid).then_inc(decay_ok, 1)
            for k in range(KC):
                x_high(0, k)
            table(ACT.Silu)
            x_high(1, 0)
            act.wait_ge(w2_in, 16)
            hi_part(w2_hi[:, :, :], w2_raw[:, :, :], wsm_hi_ok)
            x_high(1, 1)
            x_high(1, 2)
            x_high(1, 3)
            silu(0, 0)
            silu(0, 1)
            x_high(1, 4)
            x_high(1, 5)
            act.wait_ge(mid_in, 96)
            hi_part(bw_st[:, :, 0:S], bw_raw[:, :, :], wsm_hi_ok)
            hi_part(gw_hi[:, :, :], gw_raw[:, :, :], wsm_hi_ok)
            hi_part(cw_hi[:, :], cw_raw[:, :], wsm_hi_ok)
            act.wait_ge(rw2_ok, 1)
            hi_part(rw2_st[:, :, 0:E], vec[:, V_RW2:V_RW2 + RC * E].rearrange("p (c e) -> p c e", e=E), wsm_hi_ok)
            hi_part(rw1_hi[:, :, :], rw1_raw[:, :, :], wsm_hi_ok)
            silu(1, 0)
            silu(1, 1)
            normalise(0)
            xT_high(0)
            table(ACT.Sigmoid)
            w1e_high(0, 0)
            bu_high(0)
            w1e_high(0, 1)
            gates(0, 0)
            gates(0, 1)
            w1e_high(1, 0)
            normalise(1)
            xT_high(1)
            w1e_high(1, 1)
            bu_high(1)
            w1e_high(2, 0)
            gates(1, 0)
            w1e_high(2, 1)
            gates(1, 1)
            table(ACT.Gelu)
            w1e_high(3, 0)
            normalise(2)
            w1e_high(3, 1)
            xT_high(2)
            w2e_high(0, 0)
            w2e_high(0, 1)
            w2e_high(1, 0)
            router(0)
            router(1)
            normalise(3)
            router(2)
            xT_high(3)
            router(3)
            w2e_high(1, 1)
            router(4)
            router(5)
            act.wait_ge(rh_used, RC)
            nc.scalar.activation(logitsT[0:2 * E, half(0)], bank[0][0:2 * E, :], ACT.Copy).then_inc(logitsT_ok, 1)
            router(6)
            router(7)
            act.wait_ge(rh_used, 2 * RC)
            nc.scalar.activation(logitsT[0:2 * E, half(1)], bank[2][0:2 * E, :], ACT.Copy).then_inc(logitsT_ok, 1)
            act.wait_ge(shifted_ok, 2)
            nc.scalar.activation(ex[:, :, :], lg[:, :, :], ACT.Exp).then_inc(exp_ok, 1)
            table(ACT.Gelu)
            act.wait_ge(attn_ok, 2 * DC)
            for e in (2, 3):
                w2e_high(e, 0)
                w2e_high(e, 1)

            def xg_high(j, par):
                act.wait_ge(xgT_done, j + 1)
                hi_part(xg_hi[:, par], bank[3][:, 0:D].rearrange("p (c t) -> p c t", c=DC), xg_hi_ok)

            def gelu(j, par, first):
                for n in range(2):
                    act.wait_ge(hT_done, 2 * j + n + 1)
                    if not first and n == 0:
                        act.wait_ge(down_done, j - 1)
                    src = bank[6 + n][:, :].rearrange("p (c t) -> p c t", t=P)
                    nc.scalar.activation(hT_raw[:, par, 4 * n:4 * n + 4], src, ACT.Gelu)
                    nc.scalar.activation(hT_hi[:, par, 4 * n:4 * n + 4], src, ACT.Gelu).then_inc(gelu_ok, 1)

            def weigh(j, par, first):
                act.wait_ge(y_ok, j + 1)
                if not first:
                    act.wait_ge(scattered, 16 * (j - 1))
                nc.scalar.activation(y_w[:, par, :], y[:, par, :], ACT.Copy,
                                     scale=slot_w[:, bass.ds(j, 1)]).then_inc(yw_ok, 1)

            def step(i, par, lo=True):
                if lo or i + 1 < NT:
                    xg_high(i + 1, 1 - par)
                gelu(i - 1, 1 - par, False)
                weigh(i - 2, par, False)

            xg_high(0, 0)
            xg_high(1, 1)
            xg_high(2, 0)
            gelu(0, 0, True)
            xg_high(3, 1)
            gelu(1, 1, True)
            weigh(0, 0, True)
            xg_high(4, 0)
            gelu(2, 0, False)
            weigh(1, 1, True)
            with act.Fori(FULL.start, FULL.stop, 2) as i:
                step(i, 0)
                step(i + 1, 1)
            for i in range(FULL.stop, NT + 2):
                if i - 1 < NT:
                    gelu(i - 1, (i - 1) % 2, False)
                weigh(i - 2, i % 2, False)

        @block.vector
        def _(dve):
            steps = [0]
            V = nc.vector

            def then(ins):
                steps[0] += 1
                ins.then_inc(dve_step, 1)
                dve.wait_ge(dve_step, steps[0])

            def lo_part(dst, src, hi, done):
                V.tensor_tensor(dst, src, bf(hi), ALU.subtract).then_inc(done, 1)

            V.memset(zero[:, :], 0.0).then_inc(zero_ok, 1)
            then(V.memset(carry[:, :], 1.0))
            V.memset(carry[:, :].rearrange("p (b t) -> p b t", t=SEQ)[:, :, 0:1], 0.0)
            V.memset(bf(rw2_st[:, :, :]), 0.0).then_inc(rw2_ok, 1)
            then(V.memset(powers[:, :, :], 1.0))

            def x_low(hf, k):
                dve.wait_ge(x_hi_ok, hf * KC + k + 1)
                if hf == 0:
                    V.tensor_tensor(w1_lo[:, k, :], w1_raw[:, k, :], bf(w1_hi[:, k, :]), ALU.subtract)
                lo_part(x_lo[:, k, half(hf)], x_raw[:, k, half(hf)], x_hi[:, k, half(hf)], x_ok)

            def h1_low(k):
                for oc in range(DC):
                    dve.wait_ge(silu_done, k * DC + oc + 1)
                    lo_part(h1_lo[:, oc, half(k)], h1_raw[:, oc, half(k)], h1_hi[:, oc, half(k)], h1_ok)

            def normalise(n, meanwhile=None):
                k = n % 2
                gs = range(4 * k, 4 * k + 4)
                for g in gs:
                    last = V.bn_stats(stats[:, g, :], h[:, g, :])
                then(last)
                for g in gs:
                    last = V.bn_aggr(mv[:, g, :], stats[:, g, :])
                then(last)
                V.tensor_scalar(veps[:, 4 * k:4 * k + 4], mv[:, 4 * k:4 * k + 4, 1], EPS, None,
                                ALU.add).then_inc(veps_ok, 1)
                if meanwhile:
                    meanwhile()
                dve.wait_ge(rstd_ok, n + 1)
                V.scalar_tensor_tensor(shift[:, 4 * k:4 * k + 4], mv[:, 4 * k:4 * k + 4, 0], -1.0,
                                       rstd[:, 4 * k:4 * k + 4], ALU.mult, ALU.mult).then_inc(shift_ok, 1)
                for g in gs[0:2]:
                    V.tensor_scalar(xn[:, g, :], h[:, g, :], mv[:, g, 0:1], rstd[:, g:g + 1], ALU.subtract,
                                    ALU.mult).then_inc(xn_v_ok, 1)

            def xT_low(n):
                k = n % 2
                for c in range(DC):
                    dve.wait_ge(xT_hi_ok, n * DC + c + 1)
                    lo_part(xT_lo[:, c, half(k)], bank[k * DC + c][:, :], xT_hi[:, c, half(k)], xT_ok)

            def embedded(k):
                for g in range(4 * k, 4 * k + 4):
                    dve.wait_ge(tok_done, g + 1)
                    V.tensor_tensor(h[:, g, :], bank[4 + g % 4][:, 0:D], b2_bc[:, :], ALU.add).then_inc(h_ok, 1)
                dve.wait_ge(h_ok, 4 * (k + 1))

            def bu_low(k):
                dve.wait_ge(bu_hi_ok, k + 1)
                lo_part(bu_lo[:, half(k)], bank[2 * k][:, :], bu_hi[:, half(k)], bu_ok)

            def attend_sum(k, oc):
                n = k * DC + oc
                dve.wait_ge(c_done, n + 1)
                sv = scan_out[:, oc, half(k)].rearrange("p (b t) -> p b t", t=SEQ)
                then(V.tensor_tensor(sv, bank[2 * k + 1 - oc][:, :].rearrange("p (b t) -> p b t", t=SEQ),
                                     powers[:, oc, :].unsqueeze(1).broadcast_to([P, HT // SEQ, SEQ]), ALU.mult))
                then(V.tensor_tensor_scan(scan_out[:, oc, half(k)], carry[:, :], scan_out[:, oc, half(k)], 0.0,
                                          ALU.mult, ALU.add))

            def attend_gate(k, oc):
                n = k * DC + oc
                gv = gate[:, oc, half(k)].rearrange("p (b t) -> p b t", t=SEQ)
                sv = scan_out[:, oc, half(k)].rearrange("p (b t) -> p b t", t=SEQ)
                dve.wait_ge(gate_ok, n + 1)
                V.tensor_tensor(gv[:, :, 1:SEQ], gv[:, :, 1:SEQ], sv[:, :, 0:SEQ - 1], ALU.mult)
                V.memset(gv[:, :, 0:1], 0.0).then_inc(attn_ok, 1)

            def attend(k, oc):
                attend_sum(k, oc)
                attend_gate(k, oc)

            def residual(k):
                for b in range(2 * k, 2 * k + 2):
                    dve.wait_ge(attnT_done, b + 1)
                    pair = h[:, 2 * b:2 * b + 2, :].rearrange("p g n -> p (g n)")
                    V.tensor_tensor(pair, bank[4 + b][:, :], pair, ALU.add).then_inc(h2_ok, 1)
                dve.wait_ge(h2_ok, 2 * (k + 1))

            def rh_low(n):
                dve.wait_ge(rh_hi_ok, n + 1)
                lo_part(rh_lo[:, n % 4, :], rh_raw[:, n % 4, :], rh_hi[:, n % 4, :], rh_ok)

            for k in range(KC):
                x_low(0, k)
            dve.wait_ge(decay_ok, 1)
            for c in range(DC):
                V.tensor_tensor_scan(powers[:, c, 1:SEQ], decay[:, c:c + 1].broadcast_to([P, SEQ - 1]),
                                     carry[:, 1:2].broadcast_to([P, SEQ - 1]), 1.0, ALU.mult, ALU.mult)
            x_low(1, 0)
            dve.wait_ge(wsm_hi_ok, 1)
            lo_part(w2_lo[:, :, :], w2_raw[:, :, :], w2_hi[:, :, :], wsm_ok)
            x_low(1, 1)
            x_low(1, 2)
            x_low(1, 3)
            h1_low(0)
            x_low(1, 4)
            x_low(1, 5)
            dve.wait_ge(cst_in, 32)
            for a in range(2):
                V.tensor_copy(vals[:, a * G:(a + 1) * G, 0], cst[:, C_TOK1:C_TOK1 + G])
            embedded(0)
            normalise(0)
            dve.wait_ge(wsm_hi_ok, 5)
            lo_part(rw2_st[:, :, E:2 * E], vec[:, V_RW2:V_RW2 + RC * E].rearrange("p (c e) -> p c e", e=E),
                    rw2_st[:, :, 0:E], wsm_ok)
            lo_part(bw_st[:, :, S:2 * S], bw_raw[:, :, :], bw_st[:, :, 0:S], wsm_ok)
            lo_part(gw_lo[:, :, :], gw_raw[:, :, :], gw_hi[:, :, :], wsm_ok)
            lo_part(cw_lo[:, :], cw_raw[:, :], cw_hi[:, :], wsm_ok)
            h1_low(1)
            xT_low(0)
            embedded(1)
            normalise(1, lambda: bu_low(0))
            attend(0, 0)
            xT_low(1)
            attend(0, 1)
            bu_low(1)
            residual(0)
            normalise(2, lambda: attend_sum(1, 0))
            attend_gate(1, 0)
            attend(1, 1)
            xT_low(2)
            residual(1)
            normalise(3)
            rh_low(0)
            rh_low(1)
            xT_low(3)
            rh_low(2)
            for n in range(3, 2 * RC):
                rh_low(n)
            def mark(ins):
                steps[0] += 1
                ins.then_inc(dve_step, 1)
                return steps[0]

            def up(ap, n):
                return ap.unsqueeze(2).broadcast_to([P, ap.shape[1], n])

            def lead(ap, n):
                return ap.unsqueeze(1).broadcast_to([P, n, ap.shape[1]])

            def ge(ap):
                return ap.rearrange("p e g -> p g e")

            flat = lambda t: t[:, :, :].rearrange("p e g -> p (e g)")
            def choose(k):
                s = slice(4 * k, 4 * k + 4)
                n = 4
                dve.wait_ge(logits_done, k + 1)
                parts = bank[6 + k][:, 0:G * 2 * E].rearrange("p (g e) -> p g e", e=2 * E)[:, s]
                then(V.tensor_tensor(lg[:, s, :], parts[:, :, 0:E], lead(rb2_bc[:, :], n), ALU.add))
                then(V.tensor_tensor(lg[:, s, :], parts[:, :, E:2 * E], lg[:, s, :], ALU.add))
                pj = lg[:, s, :].unsqueeze(2).broadcast_to([P, n, E, E])
                pe_ = lg[:, s, :].unsqueeze(3).broadcast_to([P, n, E, E])
                V.tensor_tensor(beats[:, s, :, 0, :], pj, pe_, ALU.is_gt)
                compared = mark(V.tensor_tensor(beats[:, s, :, 1, :], pj, pe_, ALU.is_ge))
                topped = mark(V.tensor_reduce(lmax[:, s], lg[:, s, :], AX.X, ALU.max))
                dve.wait_ge(dve_step, compared)
                b4 = beats[:, s, :, :, :].rearrange("p g e k j -> p g (e k j)")
                masked = mark(V.tensor_tensor(b4, b4, lead(cst[:, C_ORDER:C_ORDER + 2 * E * E], n), ALU.mult))
                dve.wait_ge(dve_step, topped)
                V.tensor_tensor(lg[:, s, :], lg[:, s, :], up(lmax[:, s], E), ALU.subtract).then_inc(shifted_ok, 1)
                dve.wait_ge(dve_step, masked)
                then(V.tensor_reduce(rank[:, s, :], beats[:, s, :, :, :].rearrange("p g e k j -> p g e (k j)"), AX.X,
                                     ALU.add))
                then(V.tensor_scalar(ge(mask[:, :, s]), rank[:, s, :], TOPK - 0.5, None, ALU.is_lt))

            choose(0)
            choose(1)
            V.tensor_tensor_scan(flat(incl), cst[:, C_RESET:C_RESET + E * G], flat(mask), 0.0, ALU.mult,
                                 ALU.add).then_inc(mask_ok, 1)
            dve.wait_ge(exp_ok, 1)
            then(V.tensor_reduce(lsum[:, :], ex[:, :, :], AX.X, ALU.add))
            then(V.reciprocal(lrec[:, :], lsum[:, :]))
            V.tensor_tensor(pr[:, :, :], ex[:, :, :], up(lrec[:, :], E), ALU.mult)
            V.memset(tstart[:, 0:1], 0.0)
            dve.wait_ge(counts_done, 1)
            then(V.tensor_tensor(full[:, :, :], up(bank[3][:, E:2 * E], G), lead(cst[:, C_THR8:C_THR8 + G], E),
                                 ALU.is_gt))
            then(V.tensor_reduce(ntile[:, :], full[:, :, :], AX.X, ALU.add))
            then(V.tensor_tensor_scan(tstart[:, 1:E], cst[:, C_ONES:C_ONES + E - 1], ntile[:, 0:E - 1], 0.0, ALU.mult,
                                      ALU.add))
            then(V.scalar_tensor_tensor(base[:, :], tstart[:, :], float(P), bank[3][:, 0:E], ALU.mult, ALU.add))
            then(V.tensor_tensor(incl[:, :, :], incl[:, :, :], up(base[:, :], G), ALU.add))
            then(V.tensor_tensor(selpos[:, :, :], incl[:, :, :], mask[:, :, :], ALU.mult))
            top_slot = mark(V.tensor_reduce(pos2[:, 1, :], ge(selpos[:, :, :]), AX.X, ALU.max))
            summed = mark(V.tensor_reduce(psum2[:, :], ge(selpos[:, :, :]), AX.X, ALU.add))
            dve.wait_ge(dve_step, top_slot)
            is_top = mark(V.tensor_tensor(isb[:, :, :], selpos[:, :, :], lead(pos2[:, 1, :], E), ALU.is_equal))
            dve.wait_ge(dve_step, summed)
            pair = mark(V.tensor_tensor(pos2[:, 0, :], psum2[:, :], pos2[:, 1, :], ALU.subtract))
            dve.wait_ge(dve_step, is_top)
            others = mark(V.tensor_tensor(isa[:, :, :], mask[:, :, :], isb[:, :, :], ALU.subtract))
            dve.wait_ge(dve_step, pair)
            w2f = w2s[:, :, :].rearrange("p a g -> p (a g)")
            p2f = pos2[:, :, :].rearrange("p a g -> p (a g)")
            whole = mark(V.tensor_scalar(slot_no[:, :], p2f, -1.0, None, ALU.add))
            dve.wait_ge(dve_step, others)
            V.tensor_tensor(isb[:, :, :], isb[:, :, :], pr[:, :, :].rearrange("p g e -> p e g"), ALU.mult)
            weighed = mark(V.tensor_tensor(isa[:, :, :], isa[:, :, :], pr[:, :, :].rearrange("p g e -> p e g"), ALU.mult))
            dve.wait_ge(dve_step, whole)
            V.tensor_scalar(hi2[:, :], slot_no[:, :], TILE_BITS, None, ALU.logical_shift_right)
            laned = mark(V.tensor_scalar(lo2[:, :], slot_no[:, :], P - 1, None, ALU.bitwise_and))
            dve.wait_ge(dve_step, weighed)
            V.tensor_reduce(w2s[:, 0, :], ge(isa[:, :, :]), AX.X, ALU.add)
            w_ready = mark(V.tensor_reduce(w2s[:, 1, :], ge(isb[:, :, :]), AX.X, ALU.add))
            dve.wait_ge(dve_step, laned)
            V.tensor_tensor(oh_hi[:, :, :], up(hi2[:, :], NTP), lead(cst[:, C_IOTA20:C_IOTA20 + NTP], 2 * G),
                            ALU.is_equal)
            dve.wait_ge(dve_step, w_ready)
            w_high = mark(V.tensor_copy(vals[:, :, 1].bitcast(f32r), w2f))
            dve.wait_ge(dve_step, w_high)
            V.tensor_tensor(vals[:, :, 2], w2f, vals[:, :, 1], ALU.subtract).then_inc(vals_ok, 1)
            dve.wait_ge(dve_step, laned)
            iota = cst[:, C_IOTA:C_IOTA + P]
            for q in range(4):
                s = slice(q * G // 2, (q + 1) * G // 2)
                V.tensor_tensor(oh_lo[:, s, :], lead(iota, G // 2), up(lo2[:, s], P), ALU.is_equal).then_inc(onehot_ok, 1)
            then(V.tensor_tensor(reach[:, :, :], up(cst[:, C_IOTA20:C_IOTA20 + NTP], E - 1),
                                 lead(tstart[:, 1:E], NTP), ALU.is_ge))
            then(V.tensor_reduce(e_f[:, :], reach[:, :, :], AX.X, ALU.add))
            V.tensor_copy(e_of_tile[:, :], e_f[:, :]).then_inc(emap_ok, 1)
            dve.wait_ge(table_done, 1)
            then(V.tensor_copy(tab[:, :, :], bank[0][:, 0:3 * NTP].rearrange("p (k j) -> p k j", k=3)))
            V.tensor_scalar(gather_idx[:, :], tab[:, 0, :], -1.0, 0.0, ALU.add, ALU.max).then_inc(idx_ok, 1)
            V.tensor_tensor(slot_w[:, :], tab[:, 1, :], tab[:, 2, :], ALU.add)
            then(V.tensor_scalar(padz[:, :], tab[:, 0, :], 0.0, cst[:, C_PAD:C_PAD + 1], ALU.is_equal, ALU.mult))
            V.scalar_tensor_tensor(scatter_idx[:, :], tab[:, 0, :], -1.0, padz[:, :], ALU.add,
                                   ALU.add).then_inc(idx_ok, 1)
            for part in range(2):
                s = slice(4 * part, 4 * part + 4)
                dve.wait_ge(w2e_hi_ok, 2 * (E - 1) + part + 1)
                V.tensor_tensor(w2e_lo[:, E - 1, s], w2e_raw[:, E - 1, s], bf(w2e_hi[:, E - 1, s]),
                                ALU.subtract).then_inc(w2e_last_ok, 1)
            dve.wait_ge(be_in, 32)
            dve.wait_ge(emap_ok, 1)

            def evacuate(i, par, first):
                e = dve.value_load(e_of_tile[0:1, bass.ds(i, 1)], min_val=0, max_val=E - 1)
                for n in range(2):
                    dve.wait_ge(up_done, 2 * i + n + 1)
                    if not first:
                        dve.wait_ge(hT_done, 2 * i - 3 + n)
                    V.tensor_tensor(hpre[:, par, n * 512:(n + 1) * 512], bank[4 + n][:, :],
                                    be1_bc[:, bass.ds(e, 1), n * 512:(n + 1) * 512].squeeze(1), ALU.add).then_inc(hpre_ok, 1)
                    if isinstance(i, int) and i == 0 and n == 0:
                        xg_low(1, 1)

            def xg_low(j, par):
                dve.wait_ge(xg_hi_ok, j + 1)
                lo_part(xg_lo[:, par], bank[3][:, 0:D].rearrange("p (c t) -> p c t", c=DC), xg_hi[:, par], xg_ok)

            def split(j, par):
                for n in range(2):
                    dve.wait_ge(gelu_ok, 2 * j + n + 1)
                    s = slice(4 * n, 4 * n + 4)
                    lo_part(hT_lo[:, par, s], hT_raw[:, par, s], hT_hi[:, par, s], hT_ok)

            def result(j, par, first):
                e = dve.value_load(e_of_tile[0:1, bass.ds(j, 1)], min_val=0, max_val=E - 1)
                dve.wait_ge(down_done, j + 1)
                if not first:
                    dve.wait_ge(yw_ok, j - 1)
                V.tensor_tensor(y[:, par, :], bank[par][:, 0:D],
                                be2_bc[:, bass.ds(e, 1), :].squeeze(1), ALU.add).then_inc(y_ok, 1)

            def step(i, par):
                evacuate(i, par, False)
                xg_low(i + 1, 1 - par)
                split(i - 1, 1 - par)
                result(i - 2, par, False)

            xg_low(0, 0)
            for i in range(4):
                evacuate(i, i % 2, i < 2)
                if i >= 1:
                    xg_low(i + 1, (i + 1) % 2)
                if i >= 1:
                    split(i - 1, (i - 1) % 2)
                if i >= 2:
                    result(i - 2, i % 2, i - 2 < 2)
            with dve.Fori(FULL.start, FULL.stop, 2) as i:
                step(i, 0)
                step(i + 1, 1)
            for i in range(FULL.stop, NT + 2):
                if i < NT:
                    evacuate(i, i % 2, False)
                if i - 1 < NT:
                    split(i - 1, (i - 1) % 2)
                result(i - 2, i % 2, False)

        @block.tensor
        def _(pe):
            T = nc.tensor

            def three(dst, st_hi, st_lo, mv_hi, mv_lo, first, last):
                T.matmul(dst, st_hi, mv_hi, start=first, stop=False)
                T.matmul(dst, st_hi, mv_lo, start=False, stop=False)
                return T.matmul(dst, st_lo, mv_hi, start=False, stop=last)

            def keep_warm(count, b=7):
                z = zero[:, :].bitcast(mybir.dt.bfloat16)
                for _ in range(count):
                    T.matmul(bank[b][:, :], z[:, 0:P], z, start=True, stop=True)

            def embed(hf, k):
                x = slice(hf * HT, (hf + 1) * HT)
                pe.wait_ge(x_hi_ok, hf * KC + k + 1)
                for oc in range(DC):
                    T.matmul(bank[hf * DC + oc][:, :], w1_hi[:, k, oc * P:(oc + 1) * P], x_hi[:, k, x], start=k == 0,
                             stop=False)
                pe.wait_ge(x_ok, hf * KC + k + 1)
                for oc in range(DC):
                    o = slice(oc * P, (oc + 1) * P)
                    T.matmul(bank[hf * DC + oc][:, :], w1_hi[:, k, o], x_lo[:, k, x], start=False, stop=False)
                    ins = T.matmul(bank[hf * DC + oc][:, :], w1_lo[:, k, o], x_hi[:, k, x], start=False,
                                   stop=k == KC - 1)
                    if k == KC - 1:
                        ins.then_inc(embed_done, 1)

            def second_layer(k):
                for g in range(4 * k, 4 * k + 4):
                    pe.wait_ge(h1_ok, DC * (k + 1))
                    if g >= 4:
                        pe.wait_ge(h_ok, g - 3)
                    for c in range(DC):
                        ins = three(bank[4 + g % 4][:, 0:D], h1_hi[:, c, rows(g)], h1_lo[:, c, rows(g)],
                                    w2_hi[:, c, :], w2_lo[:, c, :], c == 0, c == DC - 1)
                    ins.then_inc(tok_done, 1)

            def transpose_xn(n):
                k = n % 2
                for c in range(DC):
                    for g in range(4 * k, 4 * k + 4):
                        if g % 4 < 2:
                            pe.wait_ge(xn_v_ok, 2 * n + g % 4 + 1)
                        else:
                            pe.wait_ge(xn_a_ok, 2 * n + g % 4 - 1)
                        ins = T.transpose(bank[k * DC + c][:, rows(g % 4)], xn[:, g, c * P:(c + 1) * P], ident)
                    ins.then_inc(xnT_done, 1)

            def b_proj(k):
                pe.wait_ge(xT_ok, DC * (k + 1))
                dst = bank[2 * k][:, :]
                for c in range(DC):
                    T.matmul(dst, bw_st[:, c, :], xT_hi[:, c, half(k)], start=c == 0, stop=False)
                for c in range(DC):
                    ins = T.matmul(dst, bw_st[:, c, :], xT_lo[:, c, half(k)], start=False, stop=c == DC - 1)
                ins.then_inc(bu_done, 1)

            def gate_proj(k, oc):
                o = slice(oc * P, (oc + 1) * P)
                pe.wait_ge(h_ok, 5 + 2 * k + oc)
                for c in range(DC):
                    ins = three(bank[4 + 2 * k + oc][:, :], gw_hi[:, c, o], gw_lo[:, c, o],
                                xT_hi[:, c, half(k)], xT_lo[:, c, half(k)], c == 0, c == DC - 1)
                ins.then_inc(gate_done, 1)

            def c_proj(k):
                pe.wait_ge(bu_ok, k + 1)
                for oc in range(DC):
                    o = slice(oc * P, (oc + 1) * P)
                    three(bank[2 * k + 1 - oc][:, :], cw_hi[:, o], cw_lo[:, o], bu_hi[:, half(k)], bu_lo[:, half(k)],
                          True, True).then_inc(c_done, 1)

            def turn_back(k):
                pe.wait_ge(attn_ok, DC * (k + 1))
                for g in range(4 * k, 4 * k + 4):
                    for c in range(DC):
                        ins = T.transpose(bank[4 + g // 2][:, (g % 2) * D + c * P:(g % 2) * D + (c + 1) * P],
                                          gate[:, c, rows(g)], ident)
                    if g % 2 == 1:
                        ins.then_inc(attnT_done, 1)

            def logits(n):
                k, rc = divmod(n, RC)
                pe.wait_ge(rh_ok, n + 1)
                T.matmul(bank[2 * k][:, :], rw2_st[:, rc, :], rh_hi[:, n % 4, :], start=rc == 0, stop=False)
                T.matmul(bank[2 * k][:, :], rw2_st[:, rc, :], rh_lo[:, n % 4, :], start=False,
                         stop=rc == RC - 1).then_inc(rh_used, 1)

            def router(n):
                k, rc = divmod(n, RC)
                pe.wait_ge(xT_hi_ok, 2 * DC + DC * (k + 1))
                if n >= 3:
                    pe.wait_ge(rh_hi_ok, n - 2)
                o = slice(rc * P, (rc + 1) * P)
                dst = bank[RB[n % 3]][:, :]
                for c in range(DC):
                    T.matmul(dst, rw1_hi[:, c, o], xT_hi[:, c, half(k)], start=c == 0, stop=False)
                    T.matmul(dst, rw1_lo[:, c, o], xT_hi[:, c, half(k)], start=False, stop=False)
                pe.wait_ge(xT_ok, 2 * DC + DC * (k + 1))
                for c in range(DC):
                    ins = T.matmul(dst, rw1_hi[:, c, o], xT_lo[:, c, half(k)], start=False, stop=c == DC - 1)
                ins.then_inc(router_done, 1)

            def turn_logits(k):
                pe.wait_ge(logitsT_ok, k + 1)
                pe.wait_ge(h2_ok, G // 2)
                for g in range(4 * k, 4 * k + 4):
                    ins = T.transpose(bank[6 + k][:, g * 2 * E:(g + 1) * 2 * E], logitsT[0:2 * E, rows(g)],
                                      cst[0:2 * E, C_IDENT:C_IDENT + 2 * E])
                ins.then_inc(logits_done, 1)

            pe.wait_ge(zero_ok, 1)
            keep_warm(10)
            for k in range(KC):
                embed(0, k)
            for k in range(3):
                embed(1, k)
            pe.wait_ge(wsm_ok, 1)
            second_layer(0)
            for k in range(3, KC):
                embed(1, k)
            pe.wait_ge(cst_in, 32)
            keep_warm(10, 0)
            transpose_xn(0)
            keep_warm(2, 4)
            second_layer(1)
            pe.wait_ge(wsm_ok, 5)
            b_proj(0)
            gate_proj(0, 0)
            gate_proj(0, 1)
            c_proj(0)
            keep_warm(3, 6)
            transpose_xn(1)
            keep_warm(3, 6)
            b_proj(1)
            gate_proj(1, 0)
            turn_back(0)
            gate_proj(1, 1)
            c_proj(1)
            keep_warm(8, 0)
            transpose_xn(2)
            keep_warm(8, 4)
            turn_back(1)
            pe.wait_ge(rw1_ok, 1)
            router(0)
            router(1)
            router(2)
            router(3)
            transpose_xn(3)
            logits(0)
            logits(1)
            logits(2)
            router(4)
            logits(3)
            router(5)
            logits(4)
            router(6)
            turn_logits(0)
            logits(5)
            router(7)
            logits(6)
            logits(7)
            turn_logits(1)
            pe.wait_ge(mask_ok, 1)
            T.matmul(bank[3][:, 0:E], cst[:, C_TRI:C_TRI + P], incl[:, :, G - 1], start=True, stop=True)
            T.matmul(bank[3][:, E:2 * E], cst[:, C_ONES:C_ONES + P], incl[:, :, G - 1], start=True,
                     stop=True).then_inc(counts_done, 1)
            keep_warm(16)
            for a in range(2 * G):
                pe.wait_ge(onehot_ok, 2 * a // G + 1)
                pe.wait_ge(told_ok, a // G + 1)
                ins = T.matmul(bank[0][:, 0:3 * NTP], oh_lo[:, a, :],
                               tab_rhs[:, a].rearrange("p k j -> p (k j)"), start=a == 0, stop=a == 2 * G - 1)
            ins.then_inc(table_done, 1)
            keep_warm(18)

            def turn_in(j, par, count):
                pe.wait_ge(gathered[par], 16 * count)
                if not isinstance(j, int) or j >= 1:
                    pe.wait_ge(xg_ok, j)
                for c in range(DC):
                    ins = T.transpose(bank[3][:, c * P:(c + 1) * P], xg[:, par, c * P:(c + 1) * P], ident)
                ins.then_inc(xgT_done, 1)

            def up_proj(i, par, first):
                e = pe.value_load(e_of_tile[0:1, bass.ds(i, 1)], min_val=0, max_val=E - 1)
                pe.wait_ge(xg_ok, i + 1)
                for n in range(2):
                    if not first:
                        pe.wait_ge(hpre_ok, 2 * i - 1 + n)
                    hs = slice(n * 512, (n + 1) * 512)
                    for c in range(DC):
                        w_hi = w1e_hi[:, bass.ds(e, 1), c, hs].squeeze(1)
                        w_lo = w1e_lo[:, bass.ds(e, 1), c, hs].squeeze(1)
                        ins = three(bank[4 + n][:, :], xg_hi[:, par, c, :], xg_lo[:, par, c, :], w_hi, w_lo,
                                    c == 0, c == DC - 1)
                    ins.then_inc(up_done, 1)
                    if first and n == 0:
                        turn_in(1, 1, 1)

            def turn(j, par, first):
                for n in range(2):
                    pe.wait_ge(hpre_ok, 2 * j + n + 1)
                    if not first:
                        pe.wait_ge(gelu_ok, 2 * j - 1 + n)
                    for c in range(4):
                        hc = 4 * n + c
                        ins = T.transpose(bank[6 + n][:, rows(c)], hpre[:, par, hc * P:(hc + 1) * P], ident)
                    ins.then_inc(hT_done, 1)

            def down_proj(j, par, first):
                e = pe.value_load(e_of_tile[0:1, bass.ds(j, 1)], min_val=0, max_val=E - 1)
                if not first:
                    pe.wait_ge(y_ok, j - 1)
                for hc in range(HC):
                    if hc % 4 == 0:
                        pe.wait_ge(hT_ok, 2 * j + hc // 4 + 1)
                    w_hi = w2e_hi[:, bass.ds(e, 1), hc, :].squeeze(1)
                    w_lo = w2e_lo[:, bass.ds(e, 1), hc, :].squeeze(1)
                    ins = three(bank[par][:, 0:D], hT_hi[:, par, hc, :], hT_lo[:, par, hc, :], w_hi, w_lo,
                                hc == 0, hc == HC - 1)
                ins.then_inc(down_done, 1)

            pe.wait_ge(emap_ok, 1)
            turn_in(0, 0, 1)
            pe.wait_ge(w1e_ok, DC * E)
            for i in range(4):
                up_proj(i, i % 2, i == 0)
                if i >= 1:
                    turn_in(i + 1, (i + 1) % 2, (i + 1) // 2 + 1)
                if i >= 1:
                    turn(i - 1, (i - 1) % 2, i - 1 == 0)
                if i == 2:
                    pe.wait_ge(w2e_ok, 2 * (E - 1))
                    pe.wait_ge(w2e_last_ok, 2)
                if i >= 2:
                    down_proj(i - 2, i % 2, i - 2 < 2)
            with pe.Fori(FULL.start // 2, FULL.stop // 2) as m:
                for par in range(2):
                    i = 2 * m + par
                    up_proj(i, par, False)
                    turn_in(i + 1, 1 - par, m + 1 + par)
                    turn(i - 1, 1 - par, False)
                    down_proj(i - 2, par, False)
            for i in range(FULL.stop, NT + 2):
                if i < NT:
                    up_proj(i, i % 2, False)
                if i - 1 < NT:
                    turn(i - 1, (i - 1) % 2, False)
                down_proj(i - 2, i % 2, False)


def kernel(**inputs):
    import numpy as np
    import concourse.bacc as bacc
    from concourse import mybir as mb
    from concourse.bass_utils import run_bass_kernel_spmd

    a = {k.replace("L0_", ""): np.asarray(v) for k, v in inputs.items()}
    gh = 4
    xT = a["x"].reshape(64, 3, gh, 16, gh, 16).transpose(1, 3, 5, 0, 2, 4).reshape(KC, P, TOKENS)

    def cols(v):
        return v.reshape(-1, P).T

    vecs = np.concatenate([cols(a["tok_b1"]), cols(a["attn_gate_b"]), cols(a["attn_log_decay"]), cols(a["ffn_rb1"]),
                           a["ffn_rW2"].reshape(RC, P, E).transpose(1, 0, 2).reshape(P, RC * E)], axis=1)
    p = np.arange(P)
    one = np.ones((P, 1))
    e = np.arange(E)
    consts = np.concatenate([
        np.eye(P), one * p, p[:, None] < p[None, :], np.ones((P, P)), 
        one * np.arange(NTP), one * (P * np.arange(G)), p[:, None] + P * np.arange(G) + 1, p[:, None] + TOKENS + 1,
        one * np.stack([e[None, :] > e[:, None], e[None, :] < e[:, None]], axis=1).reshape(1, -1),
        one * (np.arange(E * G) % G != 0), np.full((P, G), -0.5)], axis=1).astype(np.float32)
    arrays = {
        "xT": xT, "w1": a["tok_W1"], "w2": a["tok_W2"], "b2": a["tok_b2"], "bw": a["attn_B_w"].T, "cw": a["attn_C_w"].T,
        "gw": a["attn_gate_w"].T, "rw1": a["ffn_rW1"], "rb2": a["ffn_rb2"], "we1": a["ffn_We1"], "be1": a["ffn_be1"],
        "we2": a["ffn_We2"], "be2": a["ffn_be2"], "vecs": vecs, "consts": consts,
    }
    arrays = {k: np.ascontiguousarray(v) for k, v in arrays.items()}
    nc = bacc.Bacc("TRN2", target_bir_lowering=False, num_devices=1)
    aps = {k: nc.dram_tensor(f"in_{k}", v.shape, mb.dt.from_np(v.dtype), kind="ExternalInput").ap()
           for k, v in arrays.items()}
    out = nc.dram_tensor("out_rows", (TOKENS + P, D), mb.dt.float32, kind="ExternalOutput").ap()
    tower(nc, *(aps[k] for k in arrays), out)
    r = run_bass_kernel_spmd(nc, [{f"in_{k}": v for k, v in arrays.items()}], core_ids=[0])
    return r.results[0]["out_rows"][:TOKENS].reshape(64, SEQ, D)
```

```python
import concourse.bass as bass
from concourse import mybir

TOKENS, D, KP, S, R, E, HID = 1024, 256, 768, 64, 512, 4, 1024
SEQ = 16
P = 128
G = TOKENS // P
GH = G // 2
HT = TOKENS // 2
DC, KC, RC, HC = D // P, KP // P, R // P, HID // P
TOPK = 2
NA = -(-(TOPK * HT - E * (P - 1)) // P)
NAP = NA + NA % 2
NT = NA + (TOPK * TOKENS - NA * P + E * (P - 1)) // P
TILE_BITS = P.bit_length() - 1
NTP = NT + 1
EPS = 1e-5

C_IDENT, C_IOTA, C_TRI, C_ONES = 0, 128, 256, 384
C_IOTA20 = 512
C_THR8 = C_IOTA20 + NTP
C_TOK1 = C_THR8 + G
C_PAD = C_TOK1 + G
C_ORDER = C_PAD + 1
C_RESET = C_ORDER + E * 2 * E
C_NEGHALF = C_RESET + E * G // 2
C_COLS = C_NEGHALF + G
V_B1, V_GB, V_LD, V_RB1, V_RW2 = 0, DC, 2 * DC, 3 * DC, 3 * DC + RC
V_COLS = V_RW2 + RC * E


def tower(nc, xT, w1, w2, b2, bw, cw, gw, rw1, rb2, we1, be1, we2, be2, vecs, consts, out):
    f32, f32r, i32 = mybir.dt.float32, mybir.dt.float32r, mybir.dt.int32
    ALU = mybir.AluOpType
    ACT = mybir.ActivationFunctionType
    AX = mybir.AxisListType

    BASE = 16512
    KB = 1024

    def place(name, shape, at, dt=f32):
        return nc.alloc_sbuf_tensor_at(name, [P] + shape, dt, offset=BASE + int(at * KB))

    w1e_hi = place("w1e_hi", [E, DC, HID], 0, f32r)
    w1e_raw = place("w1e_raw", [E, DC, HID], 32)
    w1e_lo = place("w1e_lo", [E, DC, HID], 32, f32r)
    w2e_hi = place("w2e_hi", [E, HC, D], 64, f32r)
    w2e_raw = place("w2e_raw", [E, HC, D], 96)
    w2e_lo = place("w2e_lo", [E, HC, D], 96, f32r)
    x_hi = place("x_hi", [KC, TOKENS], 64, f32r)
    w1_hi = place("w1_hi", [KC, D], 88, f32r)
    x_raw = place("x_raw", [KC, TOKENS], 96)
    x_lo = place("x_lo", [KC, TOKENS], 96, f32r)
    w1_raw = place("w1_raw", [KC, D], 120)
    w1_lo = place("w1_lo", [KC, D], 120, f32r)
    bu_hi = place("bu_hi", [TOKENS], 72, f32r)
    bu_lo = place("bu_lo", [TOKENS], 76, f32r)
    scan_out = place("scan_out", [DC, TOKENS], 80)
    gate = place("gate", [DC, TOKENS], 88)
    carry = place("carry", [HT], 142)
    powers = place("powers", [DC, SEQ], 207.25)
    rh_hi = [place(f"rh_hi{i}", [HT], at, f32r) for i, at in enumerate((160.75, 162.75, 179.75))]
    rh_raw = [place(f"rh_raw{i}", [HT], at) for i, at in enumerate((164.75, 166.75, 181.75))]
    rh_lo = [place(f"rh_lo{i}", [HT], at, f32r) for i, at in enumerate((164.75, 166.75, 181.75))]
    rw2_st = place("rw2_st", [RC, 2 * E], 207.375, f32r)
    logitsT = [place(f"logitsT{i}", [HT], at) for i, at in enumerate((187.75, 191.75))]
    be1_bc = place("be1_bc", [E, HID], 128)
    be2_bc = place("be2_bc", [E, D], 144)
    b2_bc = place("b2_bc", [D], 148)
    cst = place("cst", [C_COLS], 149)
    vec = place("vec", [V_COLS], 151.75)
    rb2_bc = place("rb2_bc", [E], 151.875)
    decay = place("decay", [DC], 151.90625)
    stats = place("stats", [G, 6], 151.9375)
    mv = place("mv", [G, 2], 152.125)
    veps = place("veps", [G], 152.1875)
    rstd = place("rstd", [G], 152.21875)
    shift = place("shift", [G], 152.625)
    e_of_tile = place("e_of_tile", [NTP], 152.25, i32)
    gather_idx = place("gather_idx", [NTP], 152.34375, i32)
    scatter_idx = place("scatter_idx", [NTP], 152.4375, i32)
    slot_w = place("slot_w", [NTP], 152.53125)
    rw1_hi = place("rw1_hi", [DC, R], 152.75, f32r)
    rw1_raw = place("rw1_raw", [DC, R], 156.75)
    rw1_lo = place("rw1_lo", [DC, R], 156.75, f32r)
    gw_hi = place("gw_hi", [DC, D], 160.75, f32r)
    gw_raw = place("gw_raw", [DC, D], 162.75)
    gw_lo = place("gw_lo", [DC, D], 162.75, f32r)
    w2_hi = place("w2_hi", [DC, D], 164.75, f32r)
    w2_raw = place("w2_raw", [DC, D], 166.75)
    w2_lo = place("w2_lo", [DC, D], 166.75, f32r)
    cw_hi = place("cw_hi", [D], 168.75, f32r)
    cw_raw = place("cw_raw", [D], 169.75)
    cw_lo = place("cw_lo", [D], 169.75, f32r)
    bw_st = place("bw_st", [DC, 2 * S], 170.75, f32r)
    bw_raw = place("bw_raw", [DC, S], 206.75)
    h = place("h", [G, D], 171.75)
    xn = place("xn", [G, D], 179.75)
    h1_hi = place("h1_hi", [DC, TOKENS], 187.75, f32r)
    h1_raw = place("h1_raw", [DC, TOKENS], 195.75)
    h1_lo = place("h1_lo", [DC, TOKENS], 195.75, f32r)
    xT_hi = place("xT_hi", [DC, TOKENS], 187.75, f32r)
    xT_lo = place("xT_lo", [DC, TOKENS], 195.75, f32r)
    zero = place("zero", [D], 205.75)
    unused = place("unused", [8], 207.5)
    CH = 168.75
    lg = place("lg", [G, E], CH)
    lmax = place("lmax", [G], CH + .125)
    lsum = place("lsum", [G], CH + .15625)
    lrec = place("lrec", [G], CH + .1875)
    ex = place("ex", [G, E], CH + .25)
    pr = place("pr", [G, E], CH + .375)
    beats = place("beats", [G, E, 2, E], CH + .5)
    rank = place("rank", [G, E], CH + 1.5)
    mask = place("mask", [2, E, GH], CH + 1.625)
    incl = place("incl", [2, E, GH], CH + 1.75)

    def row(at, *specs):
        for name, shape, dt in specs:
            size = 4
            for n in shape:
                size *= n
            yield place(name, shape, at, dt)
            at += -(-size // 32) / 32

    nfull, first, count_a, rank_a, in_a, pos_a, sel_a, top_a, slot_a, hi_a, lo_a, ohhi_a, reach_a, ef_a = row(
        170.75, ("nfull", [E], f32), ("first", [E], f32), ("count_a", [E], f32), ("rank_a", [E, GH], f32),
        ("in_a", [E, GH], f32), ("pos_a", [E, GH], f32), ("sel_a", [E, GH], f32), ("top_a", [2, GH], f32),
        ("slot_a", [2 * GH], i32), ("hi_a", [2 * GH], i32), ("lo_a", [2 * GH], i32),
        ("ohhi_a", [2 * GH, NAP], f32), ("reach_a", [NA, E - 1], f32), ("ef_a", [NA], f32))
    full_a = place("full_a", [E, GH], 148)
    tabrhs_a = place("tabrhs_a", [2 * GH, NAP], 148.125, f32r)
    ohlo_a = place("ohlo_a", [2 * GH, P], 171.75, f32r)
    RT = 152.75
    (full, ntile, taken, left, start, shiftb, fix, base, reach, e_f, fixed, pos, selpos, isb, isa, psum2, pos2, w2s,
     slot_no, hi2, lo2, oh_hi, tab, padz) = row(
        RT, ("full", [E, G], f32), ("ntile", [E], f32), ("taken", [E], f32), ("left", [E], f32), ("start", [E], f32),
        ("shiftb", [E], f32), ("fix", [E], f32), ("base", [E], f32), ("reach", [NTP, E - 1], f32), ("e_f", [NTP], f32),
        ("fixed", [E, GH], f32), ("pos", [2, E, GH], f32), ("selpos", [2, E, GH], f32), ("isb", [2, E, GH], f32),
        ("isa", [2, E, GH], f32), ("psum2", [2, GH], f32), ("pos2", [2, G], f32), ("w2s", [2, G], f32),
        ("slot_no", [2 * G], i32), ("hi2", [2 * G], i32), ("lo2", [2 * G], i32), ("oh_hi", [2 * G, NTP], f32),
        ("tab", [3, NTP], f32), ("padz", [NTP], f32))
    tab_rhs = place("tab_rhs", [2 * G, 3, NTP], RT + 4, f32r)
    oh_lo = place("oh_lo", [2 * G, P], RT + 8, f32r)
    vals = place("vals", [2 * G, 3], 207.53125)
    y = place("y", [2, D], 171.75)
    y_w = place("y_w", [2, D], 173.75)
    xg_hi = place("xg_hi", [2, DC, P], 175.75, f32r)
    xg_lo = place("xg_lo", [2, DC, P], 177.75, f32r)
    hpre = place("hpre", [2, HID], 179.75)
    hT_hi = place("hT_hi", [2, HC, P], 187.75, f32r)
    hT_raw = place("hT_raw", [2, HC, P], 195.75)
    hT_lo = place("hT_lo", [2, HC, P], 195.75, f32r)
    xg = place("xg", [2, D], 203.75)

    xn_rows = nc.dram_tensor("xn_rows", [TOKENS, D], f32, kind="Internal").ap()

    bank = [nc.alloc_psum_tensor(f"bank{i}", [P, 512], f32) for i in range(8)]

    def sem(name):
        return nc.alloc_semaphore(name)

    x_in = [sem(f"x_in{n}") for n in range(2 * KC)]
    vec_in, w2_in, cst_in, mid_in, be_in = sem("vec_in"), sem("w2_in"), sem("cst_in"), sem("mid_in"), sem("be_in")
    w1e_in = [sem(f"w1e_in{e}") for e in range(E)]
    w2e_in = [sem(f"w2e_in{e}") for e in range(E)]
    x_hi_ok, x_ok = sem("x_hi_ok"), sem("x_ok")
    wsm_hi_ok, wsm_ok = sem("wsm_hi_ok"), sem("wsm_ok")
    w1e_hi_ok, w1e_ok = sem("w1e_hi_ok"), sem("w1e_ok")
    w2e_last_ok, w2e_hi_ok, w2e_ok = sem("w2e_last_ok"), sem("w2e_hi_ok"), sem("w2e_ok")
    embed_done, silu_done, h1_ok = sem("embed_done"), sem("silu_done"), sem("h1_ok")
    tok_done, h_ok = sem("tok_done"), sem("h_ok")
    veps_ok, rstd_ok, shift_ok = sem("veps_ok"), sem("rstd_ok"), sem("shift_ok")
    xn_v_ok, xn_a_ok, rw1_ok = sem("xn_v_ok"), sem("xn_a_ok"), sem("rw1_ok")
    xnT_done, xT_hi_ok, xT_ok = sem("xnT_done"), sem("xT_hi_ok"), sem("xT_ok")
    bu_done, bu_hi_ok, bu_ok = sem("bu_done"), sem("bu_hi_ok"), sem("bu_ok")
    gate_done, gate_ok, decay_ok = sem("gate_done"), sem("gate_ok"), sem("decay_ok")
    c_done, attn_ok, attnT_done, h2_ok = sem("c_done"), sem("attn_ok"), sem("attnT_done"), sem("h2_ok")
    router_done, rh_hi_ok, rh_ok = sem("router_done"), sem("rh_hi_ok"), sem("rh_ok")
    rh_pool_ok, rh_used, logitsT_ok, logits_done = sem("rh_pool_ok"), sem("rh_used"), sem("logitsT_ok"), sem("logits_done")
    shifted_ok, exp_ok, mask_ok, counts_done = sem("shifted_ok"), sem("exp_ok"), sem("mask_ok"), sem("counts_done")
    counts_a_done, onehot_a_ok, table_a_done, idx_a_ok = sem("counts_a_done"), sem("onehot_a_ok"), sem("table_a_done"), sem("idx_a_ok")
    emap_a_ok, mask_a_ok = sem("emap_a_ok"), sem("mask_a_ok")
    vals_ok, told_ok = sem("vals_ok"), sem("told_ok")
    onehot_ok, table_done, emap_ok, idx_ok = sem("onehot_ok"), sem("table_done"), sem("emap_ok"), sem("idx_ok")
    xn_stored, h2_stored, zero_ok = [sem("xn_stored0"), sem("xn_stored1")], sem("h2_stored"), sem("zero_ok")
    gathered = [sem("gathered0"), sem("gathered1")]
    xgT_done, xg_hi_ok, xg_ok = sem("xgT_done"), sem("xg_hi_ok"), sem("xg_ok")
    up_done, hpre_ok, hT_done = sem("up_done"), sem("hpre_ok"), sem("hT_done")
    gelu_ok, hT_ok, down_done = sem("gelu_ok"), sem("hT_ok"), sem("down_done")
    y_ok, yw_ok, scattered = sem("y_ok"), sem("yw_ok"), sem("scattered")
    dve_step = sem("dve_step")

    ident = cst[:, C_IDENT:C_IDENT + P]

    def half(k):
        return slice(k * HT, (k + 1) * HT)

    def rows(g):
        return slice(g * P, (g + 1) * P)

    def bf(ap):
        return ap.bitcast(f32)

    RB = (4, 5, 1)
    FULL = range(4, 18)

    with nc.Block() as block:

        @block.sync
        def _(sp):
            for k in range(KC):
                sp.dma_start(x_raw[:, k, half(0)], xT[k, :, half(0)]).then_inc(x_in[k], 16)
                sp.dma_start(w1_raw[:, k, :], w1[k * P:(k + 1) * P, :]).then_inc(x_in[k], 16)
            sp.dma_start(w2_raw[:, :, :], w2.rearrange("(c p) n -> p c n", p=P)).then_inc(w2_in, 16)
            for k in range(KC):
                sp.dma_start(x_raw[:, k, half(1)], xT[k, :, half(1)]).then_inc(x_in[KC + k], 16)
            sp.dma_start(b2_bc[:, :], b2.partition_broadcast(P)).then_inc(cst_in, 16)
            sp.dma_start(cst[:, :], consts[:, :]).then_inc(cst_in, 16)
            sp.dma_start(bw_raw[:, :, :], bw.rearrange("(c p) n -> p c n", p=P)).then_inc(mid_in, 16)
            sp.dma_start(cw_raw[0:S, :], cw[:, :]).then_inc(mid_in, 16)
            sp.dma_start(cw_raw[S:2 * S, :], cw[:, :]).then_inc(mid_in, 16)
            sp.dma_start(gw_raw[:, :, :], gw.rearrange("(c p) n -> p c n", p=P)).then_inc(mid_in, 16)
            sp.dma_start(rw1_raw[:, :, :], rw1.rearrange("(c p) n -> p c n", p=P)).then_inc(mid_in, 16)
            sp.dma_start(rb2_bc[:, :], rb2.partition_broadcast(P)).then_inc(mid_in, 16)
            for e in range(E):
                sp.dma_start(w1e_raw[:, e], we1[e].rearrange("(c p) n -> p c n", p=P)).then_inc(w1e_in[e], 16)
            sp.dma_start(be2_bc[:, :, :], be2.partition_broadcast(P)).then_inc(be_in, 16)
            sp.wait_ge(embed_done, 2 * DC)
            for e in range(E):
                sp.dma_start(w2e_raw[:, e], we2[e].rearrange("(c p) n -> p c n", p=P)).then_inc(w2e_in[e], 16)
            sp.wait_ge(zero_ok, 1)
            sp.dma_start(out[TOKENS:TOKENS + P, :], zero[:, :]).then_inc(h2_stored, 16)
            for k in range(2):
                gs = slice(4 * k, 4 * k + 4)
                sp.wait_ge(h2_ok, 2 * (k + 1))
                sp.dma_start(out[half(k), :].rearrange("(g p) n -> p g n", p=P), h[:, gs, :]).then_inc(h2_stored, 16)
                sp.wait_ge(xn_v_ok, 4 + 2 * (k + 1))
                sp.wait_ge(xn_a_ok, 4 + 2 * (k + 1))
                sp.dma_start(xn_rows[half(k), :].rearrange("(g p) n -> p g n", p=P), xn[:, gs, :]).then_inc(xn_stored[k], 16)
                if k == 0:
                    sp.wait_ge(attn_ok, 2 * DC)
                    sp.dma_start(be1_bc[:, :, :], be1.partition_broadcast(P)).then_inc(be_in, 16)

        @block.gpsimd
        def _(pool):
            def inverse_deviation(n):
                k = n % 2
                pool.wait_ge(veps_ok, n + 1)
                nc.gpsimd.tensor_tensor(rstd[:, 4 * k:4 * k + 4], veps[:, 4 * k:4 * k + 4],
                                        cst[:, C_NEGHALF:C_NEGHALF + 4], ALU.pow).then_inc(rstd_ok, 1)

            def w1e_low(e, c):
                pool.wait_ge(w1e_hi_ok, DC * e + c + 1)
                nc.gpsimd.tensor_tensor(w1e_lo[:, e, c], w1e_raw[:, e, c], bf(w1e_hi[:, e, c]),
                                        ALU.subtract).then_inc(w1e_ok, 1)

            def w2e_low(e, part):
                s = slice(4 * part, 4 * part + 4)
                pool.wait_ge(w2e_hi_ok, 2 * e + part + 1)
                nc.gpsimd.tensor_tensor(w2e_lo[:, e, s], w2e_raw[:, e, s], bf(w2e_hi[:, e, s]),
                                        ALU.subtract).then_inc(w2e_ok, 1)

            def rh_low(n):
                pool.wait_ge(rh_hi_ok, n + 1)
                nc.gpsimd.tensor_tensor(rh_lo[n % 3][:, :], rh_raw[n % 3][:, :], bf(rh_hi[n % 3][:, :]),
                                        ALU.subtract).then_inc(rh_pool_ok, 1)

            pool.wait_ge(cst_in, 32)
            inverse_deviation(0)
            pool.wait_ge(wsm_hi_ok, 6)
            nc.gpsimd.tensor_tensor(rw1_lo[:, :, :], rw1_raw[:, :, :], bf(rw1_hi[:, :, :]), ALU.subtract).then_inc(rw1_ok, 1)
            w1e_low(0, 0)
            inverse_deviation(1)
            w1e_low(0, 1)
            w1e_low(1, 0)
            w1e_low(1, 1)
            w1e_low(2, 0)
            inverse_deviation(2)
            w1e_low(2, 1)
            w1e_low(3, 0)
            inverse_deviation(3)
            w1e_low(3, 1)
            w2e_low(0, 0)
            w2e_low(0, 1)
            w2e_low(1, 0)
            rh_low(5)
            rh_low(6)
            rh_low(7)
            pool.wait_ge(idx_a_ok, 1)
            pool.wait_ge(xn_stored[0], 16)

            def gather(j):
                if j >= NT:
                    return
                if j >= 2:
                    pool.wait_ge(gathered[j % 2], 16 * (j // 2))
                    pool.wait_ge(xgT_done, j - 1)
                nc.gpsimd.indirect_dma_start(
                    out=xg[:, j % 2, :], out_offset=None, in_=xn_rows[:, :],
                    in_offset=bass.IndirectOffsetOnAxis(ap=gather_idx[:, j:j + 1], axis=0),
                ).then_inc(gathered[j % 2], 16)

            gather(0)
            gather(1)
            w2e_low(1, 1)
            w2e_low(2, 0)
            gather(2)
            w2e_low(2, 1)
            gather(3)
            pool.wait_ge(vals_ok, 1)
            for a in range(2):
                t = slice(a * G, (a + 1) * G)
                nc.gpsimd.tensor_tensor(tab_rhs[:, t, :, :], oh_hi[:, t, :].unsqueeze(2).broadcast_to([P, G, 3, NTP]),
                                        vals[:, t, :].unsqueeze(3).broadcast_to([P, G, 3, NTP]),
                                        ALU.mult).then_inc(told_ok, 1)
            gather(4)
            pool.wait_ge(idx_ok, 3)
            pool.wait_ge(xn_stored[1], 16)
            pool.wait_ge(h2_stored, 48)
            for j in range(NT):
                gather(j + 5)
                if j >= 1:
                    pool.wait_ge(scattered, 16 * j)
                pool.wait_ge(yw_ok, j + 1)
                nc.gpsimd.indirect_dma_start(
                    out=out[:, :], out_offset=bass.IndirectOffsetOnAxis(ap=scatter_idx[:, j:j + 1], axis=0),
                    in_=y_w[:, j % 2, :], in_offset=None, compute_op=ALU.add,
                ).then_inc(scattered, 16)
            pool.wait_ge(scattered, 16 * NT)

        @block.scalar
        def _(act):
            def hi_part(dst, src, done):
                nc.scalar.activation(dst, src, ACT.Copy).then_inc(done, 1)

            act.dma_start(vec[:, :], vecs[:, :]).then_inc(vec_in, 16)
            def table(i, fn):
                nc.scalar.activation(unused[:, i:i + 1], vec[:, 0:1], fn)

            def x_high(hf, k):
                n = hf * KC + k
                act.wait_ge(x_in[n], 32 if hf == 0 else 16)
                if hf == 0:
                    nc.scalar.activation(w1_hi[:, k, :], w1_raw[:, k, :], ACT.Copy)
                hi_part(x_hi[:, k, half(hf)], x_raw[:, k, half(hf)], x_hi_ok)

            def silu(k, oc):
                act.wait_ge(embed_done, k * DC + oc + 1)
                b = bank[k * DC + oc]
                nc.scalar.activation(h1_raw[:, oc, half(k)], b[:, :], ACT.Silu, bias=vec[:, V_B1 + oc:V_B1 + oc + 1])
                nc.scalar.activation(h1_hi[:, oc, half(k)], b[:, :], ACT.Silu,
                                     bias=vec[:, V_B1 + oc:V_B1 + oc + 1]).then_inc(silu_done, 1)

            def w1e_high(e, c):
                act.wait_ge(w1e_in[e], 16)
                hi_part(w1e_hi[:, e, c], w1e_raw[:, e, c], w1e_hi_ok)

            def w2e_high(e, part):
                s = slice(4 * part, 4 * part + 4)
                act.wait_ge(w2e_in[e], 16)
                hi_part(w2e_hi[:, e, s], w2e_raw[:, e, s], w2e_hi_ok)

            def normalise(n):
                act.wait_ge(shift_ok, n + 1)
                for g in range(4 * (n % 2) + 2, 4 * (n % 2) + 4):
                    nc.scalar.activation(xn[:, g, :], h[:, g, :], ACT.Identity, bias=shift[:, g:g + 1],
                                         scale=rstd[:, g:g + 1]).then_inc(xn_a_ok, 1)

            def xT_high(n):
                for c in range(DC):
                    act.wait_ge(xnT_done, n * DC + c + 1)
                    hi_part(xT_hi[:, c, half(n % 2)], bank[(n % 2) * DC + c][:, :], xT_hi_ok)

            def bu_high(k):
                act.wait_ge(bu_done, k + 1)
                hi_part(bu_hi[:, half(k)], bank[2 * k][:, :], bu_hi_ok)

            def gates(k, oc):
                act.wait_ge(gate_done, k * DC + oc + 1)
                nc.scalar.activation(gate[:, oc, half(k)], bank[4 + 2 * k + oc][:, :], ACT.Sigmoid,
                                     bias=vec[:, V_GB + oc:V_GB + oc + 1]).then_inc(gate_ok, 1)

            def router(n):
                rc = n % RC
                act.wait_ge(router_done, n + 1)
                if n == 2:
                    act.wait_ge(xn_stored[0], 16)
                if n >= 3:
                    act.wait_ge(rh_used, n - 2)
                for dst in (rh_raw[n % 3], rh_hi[n % 3]):
                    ins = nc.scalar.activation(dst[:, :], bank[RB[n % 3]][:, :], ACT.Gelu,
                                               bias=vec[:, V_RB1 + rc:V_RB1 + rc + 1])
                ins.then_inc(rh_hi_ok, 1)

            act.wait_ge(vec_in, 16)
            nc.scalar.activation(decay[:, :], vec[:, V_LD:V_LD + DC], ACT.Sigmoid).then_inc(decay_ok, 1)
            for k in range(KC):
                x_high(0, k)
            table(0, ACT.Silu)
            x_high(1, 0)
            act.wait_ge(w2_in, 16)
            hi_part(w2_hi[:, :, :], w2_raw[:, :, :], wsm_hi_ok)
            x_high(1, 1)
            x_high(1, 2)
            x_high(1, 3)
            silu(0, 0)
            silu(0, 1)
            x_high(1, 4)
            x_high(1, 5)
            act.wait_ge(mid_in, 96)
            hi_part(bw_st[:, :, 0:S], bw_raw[:, :, :], wsm_hi_ok)
            hi_part(gw_hi[:, :, :], gw_raw[:, :, :], wsm_hi_ok)
            hi_part(cw_hi[:, :], cw_raw[:, :], wsm_hi_ok)
            hi_part(rw2_st[:, :, 0:E], vec[:, V_RW2:V_RW2 + RC * E].rearrange("p (c e) -> p c e", e=E), wsm_hi_ok)
            hi_part(rw1_hi[:, :, :], rw1_raw[:, :, :], wsm_hi_ok)
            silu(1, 0)
            silu(1, 1)
            normalise(0)
            xT_high(0)
            table(1, ACT.Sigmoid)
            w1e_high(0, 0)
            bu_high(0)
            w1e_high(0, 1)
            gates(0, 0)
            gates(0, 1)
            w1e_high(1, 0)
            normalise(1)
            xT_high(1)
            w1e_high(1, 1)
            bu_high(1)
            w1e_high(2, 0)
            gates(1, 0)
            w1e_high(2, 1)
            gates(1, 1)
            table(2, ACT.Gelu)
            w1e_high(3, 0)
            normalise(2)
            w1e_high(3, 1)
            xT_high(2)
            w2e_high(0, 0)
            w2e_high(0, 1)
            w2e_high(1, 0)
            router(0)
            router(1)
            normalise(3)
            router(2)
            xT_high(3)
            router(3)
            w2e_high(1, 1)
            act.wait_ge(rh_used, RC)
            nc.scalar.activation(logitsT[0][0:2 * E, :], bank[0][0:2 * E, :], ACT.Copy).then_inc(logitsT_ok, 1)
            router(4)
            router(5)
            router(6)
            act.wait_ge(attn_ok, 2 * DC)
            w2e_high(2, 0)
            router(7)
            w2e_high(2, 1)
            w2e_high(3, 0)
            w2e_high(3, 1)
            act.wait_ge(rh_used, 2 * RC)
            nc.scalar.activation(logitsT[1][0:2 * E, :], bank[2][0:2 * E, :], ACT.Copy).then_inc(logitsT_ok, 1)
            table(3, ACT.Exp)
            act.wait_ge(shifted_ok, 2)
            nc.scalar.activation(ex[:, :, :], lg[:, :, :], ACT.Exp).then_inc(exp_ok, 1)
            act.wait_ge(h2_stored, 48)

            def xg_high(j, par):
                act.wait_ge(xgT_done, j + 1)
                hi_part(xg_hi[:, par], bank[3][:, 0:D].rearrange("p (c t) -> p c t", c=DC), xg_hi_ok)

            def gelu(j, par, first):
                for n in range(2):
                    act.wait_ge(hT_done, 2 * j + n + 1)
                    if not first and n == 0:
                        act.wait_ge(down_done, j - 1)
                    src = bank[6 + n][:, :].rearrange("p (c t) -> p c t", t=P)
                    nc.scalar.activation(hT_raw[:, par, 4 * n:4 * n + 4], src, ACT.Gelu)
                    nc.scalar.activation(hT_hi[:, par, 4 * n:4 * n + 4], src, ACT.Gelu).then_inc(gelu_ok, 1)

            def weigh(j, par, first):
                act.wait_ge(y_ok, j + 1)
                if not first:
                    act.wait_ge(scattered, 16 * (j - 1))
                nc.scalar.activation(y_w[:, par, :], y[:, par, :], ACT.Copy,
                                     scale=slot_w[:, bass.ds(j, 1)]).then_inc(yw_ok, 1)

            def step(i, par, lo=True):
                if lo or i + 1 < NT:
                    xg_high(i + 1, 1 - par)
                gelu(i - 1, 1 - par, False)
                weigh(i - 2, par, False)

            xg_high(0, 0)
            table(4, ACT.Gelu)
            xg_high(1, 1)
            xg_high(2, 0)
            gelu(0, 0, True)
            xg_high(3, 1)
            gelu(1, 1, True)
            xg_high(4, 0)
            act.wait_ge(idx_ok, 2)
            weigh(0, 0, True)
            gelu(2, 0, False)
            weigh(1, 1, True)
            with act.Fori(FULL.start, FULL.stop, 2) as i:
                step(i, 0)
                step(i + 1, 1)
            for i in range(FULL.stop, NT + 2):
                if i - 1 < NT:
                    gelu(i - 1, (i - 1) % 2, False)
                weigh(i - 2, i % 2, False)

        @block.vector
        def _(dve):
            steps = [0]
            V = nc.vector

            def then(ins):
                steps[0] += 1
                ins.then_inc(dve_step, 1)
                dve.wait_ge(dve_step, steps[0])

            def lo_part(dst, src, hi, done):
                V.tensor_tensor(dst, src, bf(hi), ALU.subtract).then_inc(done, 1)

            V.memset(zero[:, :], 0.0).then_inc(zero_ok, 1)
            then(V.memset(carry[:, :], 1.0))
            V.memset(carry[:, :].rearrange("p (b t) -> p b t", t=SEQ)[:, :, 0:1], 0.0)
            then(V.memset(powers[:, :, :], 1.0))

            def x_low(hf, k):
                dve.wait_ge(x_hi_ok, hf * KC + k + 1)
                if hf == 0:
                    V.tensor_tensor(w1_lo[:, k, :], w1_raw[:, k, :], bf(w1_hi[:, k, :]), ALU.subtract)
                lo_part(x_lo[:, k, half(hf)], x_raw[:, k, half(hf)], x_hi[:, k, half(hf)], x_ok)

            def h1_low(k):
                for oc in range(DC):
                    dve.wait_ge(silu_done, k * DC + oc + 1)
                    lo_part(h1_lo[:, oc, half(k)], h1_raw[:, oc, half(k)], h1_hi[:, oc, half(k)], h1_ok)

            def normalise(n, meanwhile=None):
                k = n % 2
                gs = range(4 * k, 4 * k + 4)
                for g in gs:
                    last = V.bn_stats(stats[:, g, :], h[:, g, :])
                then(last)
                for g in gs:
                    last = V.bn_aggr(mv[:, g, :], stats[:, g, :])
                then(last)
                V.tensor_scalar(veps[:, 4 * k:4 * k + 4], mv[:, 4 * k:4 * k + 4, 1], EPS, None,
                                ALU.add).then_inc(veps_ok, 1)
                if meanwhile:
                    meanwhile()
                dve.wait_ge(rstd_ok, n + 1)
                V.scalar_tensor_tensor(shift[:, 4 * k:4 * k + 4], mv[:, 4 * k:4 * k + 4, 0], -1.0,
                                       rstd[:, 4 * k:4 * k + 4], ALU.mult, ALU.mult).then_inc(shift_ok, 1)
                for g in gs[0:2]:
                    V.tensor_scalar(xn[:, g, :], h[:, g, :], mv[:, g, 0:1], rstd[:, g:g + 1], ALU.subtract,
                                    ALU.mult).then_inc(xn_v_ok, 1)

            def xT_low(n):
                k = n % 2
                for c in range(DC):
                    dve.wait_ge(xT_hi_ok, n * DC + c + 1)
                    lo_part(xT_lo[:, c, half(k)], bank[k * DC + c][:, :], xT_hi[:, c, half(k)], xT_ok)

            def embedded(k):
                for g in range(4 * k, 4 * k + 4):
                    dve.wait_ge(tok_done, g + 1)
                    V.tensor_tensor(h[:, g, :], bank[4 + g % 4][:, 0:D], b2_bc[:, :], ALU.add).then_inc(h_ok, 1)
                dve.wait_ge(h_ok, 4 * (k + 1))

            def bu_low(k):
                dve.wait_ge(bu_hi_ok, k + 1)
                lo_part(bu_lo[:, half(k)], bank[2 * k][:, :], bu_hi[:, half(k)], bu_ok)

            def attend_sum(k, oc):
                n = k * DC + oc
                dve.wait_ge(c_done, n + 1)
                sv = scan_out[:, oc, half(k)].rearrange("p (b t) -> p b t", t=SEQ)
                then(V.tensor_tensor(sv, bank[2 * k + 1 - oc][:, :].rearrange("p (b t) -> p b t", t=SEQ),
                                     powers[:, oc, :].unsqueeze(1).broadcast_to([P, HT // SEQ, SEQ]), ALU.mult))
                then(V.tensor_tensor_scan(scan_out[:, oc, half(k)], carry[:, :], scan_out[:, oc, half(k)], 0.0,
                                          ALU.mult, ALU.add))

            def attend_gate(k, oc):
                n = k * DC + oc
                gv = gate[:, oc, half(k)].rearrange("p (b t) -> p b t", t=SEQ)
                sv = scan_out[:, oc, half(k)].rearrange("p (b t) -> p b t", t=SEQ)
                dve.wait_ge(gate_ok, n + 1)
                V.tensor_tensor(gv[:, :, 1:SEQ], gv[:, :, 1:SEQ], sv[:, :, 0:SEQ - 1], ALU.mult)
                V.memset(gv[:, :, 0:1], 0.0).then_inc(attn_ok, 1)

            def attend(k, oc):
                attend_sum(k, oc)
                attend_gate(k, oc)

            def residual(k):
                for b in range(2 * k, 2 * k + 2):
                    dve.wait_ge(attnT_done, b + 1)
                    pair = h[:, 2 * b:2 * b + 2, :].rearrange("p g n -> p (g n)")
                    V.tensor_tensor(pair, bank[4 + b][:, :], pair, ALU.add).then_inc(h2_ok, 1)
                dve.wait_ge(h2_ok, 2 * (k + 1))

            def rh_low(n):
                dve.wait_ge(rh_hi_ok, n + 1)
                lo_part(rh_lo[n % 3][:, :], rh_raw[n % 3][:, :], rh_hi[n % 3][:, :], rh_ok)

            for k in range(KC):
                x_low(0, k)
            dve.wait_ge(decay_ok, 1)
            for c in range(DC):
                V.tensor_tensor_scan(powers[:, c, 1:SEQ], decay[:, c:c + 1].broadcast_to([P, SEQ - 1]),
                                     carry[:, 1:2].broadcast_to([P, SEQ - 1]), 1.0, ALU.mult, ALU.mult)
            x_low(1, 0)
            dve.wait_ge(wsm_hi_ok, 1)
            lo_part(w2_lo[:, :, :], w2_raw[:, :, :], w2_hi[:, :, :], wsm_ok)
            x_low(1, 1)
            x_low(1, 2)
            x_low(1, 3)
            h1_low(0)
            x_low(1, 4)
            x_low(1, 5)
            dve.wait_ge(cst_in, 32)
            for a in range(2):
                V.tensor_copy(vals[:, a * G:(a + 1) * G, 0], cst[:, C_TOK1:C_TOK1 + G])
            embedded(0)
            normalise(0)
            dve.wait_ge(wsm_hi_ok, 5)
            lo_part(rw2_st[:, :, E:2 * E], vec[:, V_RW2:V_RW2 + RC * E].rearrange("p (c e) -> p c e", e=E),
                    rw2_st[:, :, 0:E], wsm_ok)
            lo_part(bw_st[:, :, S:2 * S], bw_raw[:, :, :], bw_st[:, :, 0:S], wsm_ok)
            lo_part(gw_lo[:, :, :], gw_raw[:, :, :], gw_hi[:, :, :], wsm_ok)
            lo_part(cw_lo[:, :], cw_raw[:, :], cw_hi[:, :], wsm_ok)
            h1_low(1)
            xT_low(0)
            embedded(1)
            normalise(1, lambda: bu_low(0))
            attend(0, 0)
            xT_low(1)
            attend(0, 1)
            bu_low(1)
            residual(0)
            normalise(2, lambda: attend_sum(1, 0))
            attend_gate(1, 0)
            attend(1, 1)
            xT_low(2)
            residual(1)
            def mark(ins):
                steps[0] += 1
                ins.then_inc(dve_step, 1)
                return steps[0]

            def up(ap, n):
                return ap.unsqueeze(2).broadcast_to([P, ap.shape[1], n])

            def lead(ap, n):
                return ap.unsqueeze(1).broadcast_to([P, n, ap.shape[1]])

            def ge(ap):
                return ap.rearrange("p e g -> p g e")

            def flat(ap):
                return ap.rearrange("p e g -> p (e g)")

            def choose(k):
                s = slice(4 * k, 4 * k + 4)
                n = 4
                dve.wait_ge(logits_done, k + 1)
                parts = bank[(6, 2)[k]][:, 0:G * 2 * E].rearrange("p (g e) -> p g e", e=2 * E)[:, s]
                then(V.tensor_tensor(lg[:, s, :], parts[:, :, 0:E], lead(rb2_bc[:, :], n), ALU.add))
                then(V.tensor_tensor(lg[:, s, :], parts[:, :, E:2 * E], lg[:, s, :], ALU.add))
                pj = lg[:, s, :].unsqueeze(2).broadcast_to([P, n, E, E])
                pe_ = lg[:, s, :].unsqueeze(3).broadcast_to([P, n, E, E])
                V.tensor_tensor(beats[:, s, :, 0, :], pj, pe_, ALU.is_gt)
                compared = mark(V.tensor_tensor(beats[:, s, :, 1, :], pj, pe_, ALU.is_ge))
                topped = mark(V.tensor_reduce(lmax[:, s], lg[:, s, :], AX.X, ALU.max))
                dve.wait_ge(dve_step, compared)
                b4 = beats[:, s, :, :, :].rearrange("p g e k j -> p g (e k j)")
                masked = mark(V.tensor_tensor(b4, b4, lead(cst[:, C_ORDER:C_ORDER + 2 * E * E], n), ALU.mult))
                dve.wait_ge(dve_step, topped)
                V.tensor_tensor(lg[:, s, :], lg[:, s, :], up(lmax[:, s], E), ALU.subtract).then_inc(shifted_ok, 1)
                dve.wait_ge(dve_step, masked)
                then(V.tensor_reduce(rank[:, s, :], beats[:, s, :, :, :].rearrange("p g e k j -> p g e (k j)"), AX.X,
                                     ALU.add))
                then(V.tensor_scalar(ge(mask[:, k]), rank[:, s, :], TOPK - 0.5, None, ALU.is_lt))

            def count_up(k, done):
                V.tensor_tensor_scan(flat(incl[:, k]), cst[:, C_RESET:C_RESET + E * GH], flat(mask[:, k]), 0.0, ALU.mult,
                                     ALU.add).then_inc(done, 1)

            def first_positions():
                V.memset(first[:, 0:1], 0.0)
                dve.wait_ge(counts_a_done, 1)
                low, total = bank[7][:, 0:E], bank[7][:, E:2 * E]
                counted = mark(V.tensor_tensor(full_a[:, :, :], up(total, GH), lead(cst[:, C_THR8 + 1:C_THR8 + 1 + GH], E),
                                               ALU.is_ge))
                ranked = mark(V.tensor_tensor(rank_a[:, :, :], incl[:, 0], up(low, GH), ALU.add))
                V.tensor_copy(count_a[:, :], total)
                dve.wait_ge(dve_step, counted)
                then(V.tensor_reduce(nfull[:, :], full_a[:, :, :], AX.X, ALU.add))
                summed = mark(V.tensor_tensor_scan(first[:, 1:E], cst[:, C_ONES:C_ONES + E - 1], nfull[:, 0:E - 1], 0.0,
                                                   ALU.mult, ALU.add))
                dve.wait_ge(dve_step, ranked)
                inside = mark(V.scalar_tensor_tensor(in_a[:, :, :], up(nfull[:, :], GH), float(P), rank_a[:, :, :],
                                                     ALU.mult, ALU.is_ge))
                dve.wait_ge(dve_step, summed)
                placed = mark(V.scalar_tensor_tensor(pos_a[:, :, :], up(first[:, :], GH), float(P), rank_a[:, :, :],
                                                     ALU.mult, ALU.add))
                dve.wait_ge(dve_step, inside)
                then(V.tensor_tensor(in_a[:, :, :], in_a[:, :, :], mask[:, 0], ALU.mult))
                dve.wait_ge(dve_step, placed)
                then(V.tensor_tensor(sel_a[:, :, :], in_a[:, :, :], pos_a[:, :, :], ALU.mult))

            def first_slots():
                V.tensor_reduce(top_a[:, 1, :], ge(sel_a[:, :, :]), AX.X, ALU.max)
                then(V.tensor_reduce(top_a[:, 0, :], ge(sel_a[:, :, :]), AX.X, ALU.add))
                then(V.tensor_tensor(top_a[:, 0, :], top_a[:, 0, :], top_a[:, 1, :], ALU.subtract))
                then(V.tensor_scalar(slot_a[:, :], top_a[:, :, :].rearrange("p a g -> p (a g)"), -1.0, None, ALU.add))
                V.tensor_scalar(hi_a[:, :], slot_a[:, :], TILE_BITS, None, ALU.logical_shift_right)
                then(V.tensor_scalar(lo_a[:, :], slot_a[:, :], P - 1, None, ALU.bitwise_and))
                then(V.tensor_tensor(ohhi_a[:, :, :], up(hi_a[:, :], NAP), lead(cst[:, C_IOTA20:C_IOTA20 + NAP], 2 * GH),
                                     ALU.is_equal))
                V.tensor_tensor(tabrhs_a[:, :, :].rearrange("p (a g) j -> p a g j", a=2),
                                ohhi_a[:, :, :].rearrange("p (a g) j -> p a g j", a=2),
                                cst[:, C_TOK1:C_TOK1 + GH].unsqueeze(1).unsqueeze(3).broadcast_to([P, 2, GH, NAP]),
                                ALU.mult)
                dve.wait_ge(h2_stored, 32)
                for a in range(2):
                    s = slice(a * GH, (a + 1) * GH)
                    V.tensor_tensor(ohlo_a[:, s, :], lead(cst[:, C_IOTA:C_IOTA + P], GH), up(lo_a[:, s], P),
                                    ALU.is_equal).then_inc(onehot_a_ok, 1)

            def first_tiles():
                then(V.tensor_tensor(reach_a[:, :, :], up(cst[:, C_IOTA20:C_IOTA20 + NA], E - 1),
                                     lead(first[:, 1:E], NA), ALU.is_ge))
                then(V.tensor_reduce(ef_a[:, :], reach_a[:, :, :], AX.X, ALU.add))
                V.tensor_copy(e_of_tile[:, 0:NA], ef_a[:, :]).then_inc(emap_a_ok, 1)
                dve.wait_ge(table_a_done, 1)
                for idx in (gather_idx, scatter_idx):
                    V.tensor_scalar(idx[:, 0:NA], bank[0][:, 0:NA], -1.0, None, ALU.add).then_inc(idx_a_ok, 1)

            def second_weights():
                dve.wait_ge(exp_ok, 1)
                then(V.tensor_reduce(lsum[:, :], ex[:, :, :], AX.X, ALU.add))
                then(V.reciprocal(lrec[:, :], lsum[:, :]))
                V.tensor_tensor(pr[:, :, :], ex[:, :, :], up(lrec[:, :], E), ALU.mult)
                V.memset(start[:, 0:1], 0.0)
                then(V.tensor_scalar(taken[:, :], first[:, :], -1.0, float(NA), ALU.mult, ALU.add))
                then(V.scalar_tensor_tensor(taken[:, :], taken[:, :], 0.0, nfull[:, :], ALU.max, ALU.min))

            def second_starts():
                dve.wait_ge(counts_done, 1)
                total = bank[2][:, E:2 * E]
                then(V.tensor_tensor(full[:, :, :], up(total, G), lead(cst[:, C_THR8:C_THR8 + G], E), ALU.is_gt))
                then(V.tensor_reduce(ntile[:, :], full[:, :, :], AX.X, ALU.add))
                then(V.tensor_tensor(left[:, :], ntile[:, :], taken[:, :], ALU.subtract))
                then(V.tensor_tensor_scan(start[:, 1:E], cst[:, C_ONES:C_ONES + E - 1], left[:, 0:E - 1], 0.0, ALU.mult,
                                          ALU.add))
                then(V.tensor_tensor(shiftb[:, :], start[:, :], taken[:, :], ALU.subtract))
                then(V.tensor_scalar(shiftb[:, :], shiftb[:, :], float(P), float(P * NA), ALU.mult, ALU.add))

            def second_positions():
                low = bank[2][:, 0:E]
                V.scalar_tensor_tensor(fix[:, :], first[:, :], float(P), shiftb[:, :], ALU.mult, ALU.subtract)
                V.scalar_tensor_tensor(fixed[:, :, :], up(taken[:, :], GH), float(P), rank_a[:, :, :], ALU.mult, ALU.is_ge)
                V.tensor_tensor(pos[:, 0], rank_a[:, :, :], up(shiftb[:, :], GH), ALU.add)
                then(V.tensor_tensor(base[:, :], low, count_a[:, :], ALU.add))
                V.tensor_tensor(fixed[:, :, :], fixed[:, :, :], up(fix[:, :], GH), ALU.mult)
                then(V.tensor_tensor(base[:, :], base[:, :], shiftb[:, :], ALU.add))
                V.tensor_tensor(pos[:, 0], pos[:, 0], fixed[:, :, :], ALU.add)
                then(V.tensor_tensor(pos[:, 1], incl[:, 1], up(base[:, :], GH), ALU.add))
                allf = "p h e g -> p (h e g)"
                then(V.tensor_tensor(selpos[:, :, :, :].rearrange(allf), pos[:, :, :, :].rearrange(allf),
                                     mask[:, :, :, :].rearrange(allf), ALU.mult))

            w2f = w2s[:, :, :].rearrange("p a g -> p (a g)")

            def second_slots():
                byg = "p h e g -> p h g e"
                top2 = pos2[:, 1, :].rearrange("p (h g) -> p h g", h=2)
                V.tensor_reduce(top2, selpos[:, :, :, :].rearrange(byg), AX.X, ALU.max)
                then(V.tensor_reduce(psum2[:, :, :], selpos[:, :, :, :].rearrange(byg), AX.X, ALU.add))
                V.tensor_tensor(isb[:, :, :, :], selpos[:, :, :, :],
                                top2.unsqueeze(2).broadcast_to([P, 2, E, GH]), ALU.is_equal)
                then(V.tensor_tensor(pos2[:, 0, :], psum2[:, :, :].rearrange("p h g -> p (h g)"), pos2[:, 1, :],
                                     ALU.subtract))
                V.tensor_tensor(isa[:, :, :, :], mask[:, :, :, :], isb[:, :, :, :], ALU.subtract)
                then(V.tensor_scalar(slot_no[:, :], pos2[:, :, :].rearrange("p a g -> p (a g)"), -1.0, None, ALU.add))
                prob = pr[:, :, :].rearrange("p (h g) e -> p h e g", h=2)
                V.tensor_scalar(hi2[:, :], slot_no[:, :], TILE_BITS, None, ALU.logical_shift_right)
                V.tensor_scalar(lo2[:, :], slot_no[:, :], P - 1, None, ALU.bitwise_and)
                V.tensor_tensor(isb[:, :, :, :], isb[:, :, :, :], prob, ALU.mult)
                then(V.tensor_tensor(isa[:, :, :, :], isa[:, :, :, :], prob, ALU.mult))
                for a, side in enumerate((isa, isb)):
                    last = V.tensor_reduce(w2s[:, a, :].rearrange("p (h g) -> p h g", h=2),
                                           side[:, :, :, :].rearrange(byg), AX.X, ALU.add)
                then(last)
                V.tensor_tensor(oh_hi[:, :, :], up(hi2[:, :], NTP), lead(cst[:, C_IOTA20:C_IOTA20 + NTP], 2 * G),
                                ALU.is_equal)
                then(V.tensor_copy(vals[:, :, 1].bitcast(f32r), w2f))
                V.tensor_tensor(vals[:, :, 2], w2f, vals[:, :, 1], ALU.subtract).then_inc(vals_ok, 1)

            def second_lanes(q):
                s = slice(q * G // 2, (q + 1) * G // 2)
                V.tensor_tensor(oh_lo[:, s, :], lead(cst[:, C_IOTA:C_IOTA + P], G // 2), up(lo2[:, s], P),
                                ALU.is_equal).then_inc(onehot_ok, 1)

            def second_map():
                then(V.tensor_scalar(start[:, :], start[:, :], float(NA), None, ALU.add))
                then(V.tensor_tensor(reach[:, :, :], up(cst[:, C_IOTA20:C_IOTA20 + NTP], E - 1),
                                     lead(start[:, 1:E], NTP), ALU.is_ge))
                then(V.tensor_reduce(e_f[:, :], reach[:, :, :], AX.X, ALU.add))
                V.tensor_copy(e_of_tile[:, NA:NTP], e_f[:, NA:NTP]).then_inc(emap_ok, 1)

            def second_tiles():
                dve.wait_ge(table_done, 1)
                then(V.tensor_copy(tab[:, :, :], bank[2][:, 0:3 * NTP].rearrange("p (k j) -> p k j", k=3)))
                V.tensor_scalar(gather_idx[:, NA:NTP], tab[:, 0, NA:NTP], -1.0, 0.0, ALU.add, ALU.max).then_inc(idx_ok, 1)
                V.tensor_tensor(slot_w[:, :], tab[:, 1, :], tab[:, 2, :], ALU.add).then_inc(idx_ok, 1)
                then(V.tensor_scalar(padz[:, :], tab[:, 0, :], 0.0, cst[:, C_PAD:C_PAD + 1], ALU.is_equal, ALU.mult))
                V.scalar_tensor_tensor(scatter_idx[:, NA:NTP], tab[:, 0, NA:NTP], -1.0, padz[:, NA:NTP], ALU.add,
                                       ALU.add).then_inc(idx_ok, 1)

            normalise(3, lambda: (rh_low(0), rh_low(1)))
            rh_low(2)
            xT_low(3)
            rh_low(3)
            choose(0)
            count_up(0, mask_a_ok)
            rh_low(4)
            first_positions()
            first_slots()
            first_tiles()
            for part in range(2):
                s = slice(4 * part, 4 * part + 4)
                dve.wait_ge(w2e_hi_ok, 2 * (E - 1) + part + 1)
                lo_part(w2e_lo[:, E - 1, s], w2e_raw[:, E - 1, s], w2e_hi[:, E - 1, s], w2e_last_ok)
            dve.wait_ge(be_in, 32)
            dve.wait_ge(emap_a_ok, 1)
            dve.wait_ge(xn_stored[1], 16)
            def expert_of(i):
                return dve.value_load(e_of_tile[0:1, bass.ds(i, 1)], min_val=0, max_val=E - 1)

            def evacuate(i, par, first, e, between=None):
                for n in range(2):
                    dve.wait_ge(up_done, 2 * i + n + 1)
                    if not first:
                        dve.wait_ge(hT_done, 2 * i - 3 + n)
                    V.tensor_tensor(hpre[:, par, n * 512:(n + 1) * 512], bank[4 + n][:, :],
                                    be1_bc[:, bass.ds(e, 1), n * 512:(n + 1) * 512].squeeze(1), ALU.add).then_inc(hpre_ok, 1)
                    if n == 0 and between:
                        between()

            def xg_low(j, par):
                dve.wait_ge(xg_hi_ok, j + 1)
                lo_part(xg_lo[:, par], bank[3][:, 0:D].rearrange("p (c t) -> p c t", c=DC), xg_hi[:, par], xg_ok)

            def split(j, par):
                for n in range(2):
                    dve.wait_ge(gelu_ok, 2 * j + n + 1)
                    s = slice(4 * n, 4 * n + 4)
                    lo_part(hT_lo[:, par, s], hT_raw[:, par, s], hT_hi[:, par, s], hT_ok)

            def result(j, par, first, e):
                dve.wait_ge(down_done, j + 1)
                if not first:
                    dve.wait_ge(yw_ok, j - 1)
                V.tensor_tensor(y[:, par, :], bank[par][:, 0:D],
                                be2_bc[:, bass.ds(e, 1), :].squeeze(1), ALU.add).then_inc(y_ok, 1)

            def step(i, par):
                evacuate(i, par, False, expert_of(i))
                xg_low(i + 1, 1 - par)
                split(i - 1, 1 - par)
                result(i - 2, par, False, expert_of(i - 2))

            e0, e1 = expert_of(0), expert_of(1)
            choose(1)
            count_up(1, mask_ok)
            xg_low(0, 0)
            second_weights()
            evacuate(0, 0, True, e0, lambda: xg_low(1, 1))
            second_starts()
            evacuate(1, 1, True, e1)
            xg_low(2, 0)
            second_positions()
            split(0, 0)
            second_slots()
            evacuate(2, 0, False, expert_of(2))
            xg_low(3, 1)
            second_lanes(0)
            second_lanes(1)
            split(1, 1)
            result(0, 0, True, e0)
            second_lanes(2)
            second_lanes(3)
            second_map()
            evacuate(3, 1, False, expert_of(3))
            second_tiles()
            xg_low(4, 0)
            split(2, 0)
            result(1, 1, True, e1)
            with dve.Fori(FULL.start, FULL.stop, 2) as i:
                step(i, 0)
                step(i + 1, 1)
            for i in range(FULL.stop, NT + 2):
                if i < NT:
                    evacuate(i, i % 2, False, expert_of(i))
                if i - 1 < NT:
                    split(i - 1, (i - 1) % 2)
                result(i - 2, i % 2, False, expert_of(i - 2))

        @block.tensor
        def _(pe):
            T = nc.tensor

            def three(dst, st_hi, st_lo, mv_hi, mv_lo, first, last):
                T.matmul(dst, st_hi, mv_hi, start=first, stop=False)
                T.matmul(dst, st_hi, mv_lo, start=False, stop=False)
                return T.matmul(dst, st_lo, mv_hi, start=False, stop=last)

            def keep_warm(count, b=7):
                z = zero[:, :].bitcast(mybir.dt.bfloat16)
                for _ in range(count):
                    T.matmul(bank[b][:, :], z[:, 0:P], z, start=True, stop=True)

            def embed(hf, k):
                x = slice(hf * HT, (hf + 1) * HT)
                pe.wait_ge(x_hi_ok, hf * KC + k + 1)
                for oc in range(DC):
                    T.matmul(bank[hf * DC + oc][:, :], w1_hi[:, k, oc * P:(oc + 1) * P], x_hi[:, k, x], start=k == 0,
                             stop=False)
                pe.wait_ge(x_ok, hf * KC + k + 1)
                for oc in range(DC):
                    o = slice(oc * P, (oc + 1) * P)
                    T.matmul(bank[hf * DC + oc][:, :], w1_hi[:, k, o], x_lo[:, k, x], start=False, stop=False)
                    ins = T.matmul(bank[hf * DC + oc][:, :], w1_lo[:, k, o], x_hi[:, k, x], start=False,
                                   stop=k == KC - 1)
                    if k == KC - 1:
                        ins.then_inc(embed_done, 1)

            def second_layer(k):
                for g in range(4 * k, 4 * k + 4):
                    pe.wait_ge(h1_ok, DC * (k + 1))
                    if g >= 4:
                        pe.wait_ge(h_ok, g - 3)
                    for c in range(DC):
                        ins = three(bank[4 + g % 4][:, 0:D], h1_hi[:, c, rows(g)], h1_lo[:, c, rows(g)],
                                    w2_hi[:, c, :], w2_lo[:, c, :], c == 0, c == DC - 1)
                    ins.then_inc(tok_done, 1)

            def transpose_xn(n):
                k = n % 2
                for c in range(DC):
                    for g in range(4 * k, 4 * k + 4):
                        if g % 4 < 2:
                            pe.wait_ge(xn_v_ok, 2 * n + g % 4 + 1)
                        else:
                            pe.wait_ge(xn_a_ok, 2 * n + g % 4 - 1)
                        ins = T.transpose(bank[k * DC + c][:, rows(g % 4)], xn[:, g, c * P:(c + 1) * P], ident)
                    ins.then_inc(xnT_done, 1)

            def b_proj(k):
                pe.wait_ge(xT_ok, DC * (k + 1))
                dst = bank[2 * k][:, :]
                for c in range(DC):
                    T.matmul(dst, bw_st[:, c, :], xT_hi[:, c, half(k)], start=c == 0, stop=False)
                for c in range(DC):
                    ins = T.matmul(dst, bw_st[:, c, :], xT_lo[:, c, half(k)], start=False, stop=c == DC - 1)
                ins.then_inc(bu_done, 1)

            def gate_proj(k, oc):
                o = slice(oc * P, (oc + 1) * P)
                pe.wait_ge(h_ok, 5 + 2 * k + oc)
                for c in range(DC):
                    ins = three(bank[4 + 2 * k + oc][:, :], gw_hi[:, c, o], gw_lo[:, c, o],
                                xT_hi[:, c, half(k)], xT_lo[:, c, half(k)], c == 0, c == DC - 1)
                ins.then_inc(gate_done, 1)

            def c_proj(k):
                pe.wait_ge(bu_ok, k + 1)
                for oc in range(DC):
                    o = slice(oc * P, (oc + 1) * P)
                    three(bank[2 * k + 1 - oc][:, :], cw_hi[:, o], cw_lo[:, o], bu_hi[:, half(k)], bu_lo[:, half(k)],
                          True, True).then_inc(c_done, 1)

            def turn_back(k):
                pe.wait_ge(attn_ok, DC * (k + 1))
                for g in range(4 * k, 4 * k + 4):
                    for c in range(DC):
                        ins = T.transpose(bank[4 + g // 2][:, (g % 2) * D + c * P:(g % 2) * D + (c + 1) * P],
                                          gate[:, c, rows(g)], ident)
                    if g % 2 == 1:
                        ins.then_inc(attnT_done, 1)

            def logits(n):
                k, rc = divmod(n, RC)
                if n < 5:
                    pe.wait_ge(rh_ok, n + 1)
                else:
                    pe.wait_ge(rh_pool_ok, n - 4)
                T.matmul(bank[2 * k][0:2 * E, :], rw2_st[:, rc, :], rh_hi[n % 3][:, :], start=rc == 0, stop=False)
                T.matmul(bank[2 * k][0:2 * E, :], rw2_st[:, rc, :], rh_lo[n % 3][:, :], start=False,
                         stop=rc == RC - 1).then_inc(rh_used, 1)

            def router(n, between=None):
                k, rc = divmod(n, RC)
                pe.wait_ge(xT_hi_ok, 2 * DC + DC * (k + 1))
                if n >= 3:
                    pe.wait_ge(rh_hi_ok, n - 2)
                o = slice(rc * P, (rc + 1) * P)
                dst = bank[RB[n % 3]][:, :]
                for c in range(DC):
                    T.matmul(dst, rw1_hi[:, c, o], xT_hi[:, c, half(k)], start=c == 0, stop=False)
                    T.matmul(dst, rw1_lo[:, c, o], xT_hi[:, c, half(k)], start=False, stop=False)
                if between:
                    between()
                pe.wait_ge(xT_ok, 2 * DC + DC * (k + 1))
                for c in range(DC):
                    ins = T.matmul(dst, rw1_hi[:, c, o], xT_lo[:, c, half(k)], start=False, stop=c == DC - 1)
                ins.then_inc(router_done, 1)

            def turn_logits(k):
                pe.wait_ge(logitsT_ok, k + 1)
                pe.wait_ge(h2_ok, G // 2)
                for g in range(4 * k, 4 * k + 4):
                    ins = T.transpose(bank[(6, 2)[k]][:, g * 2 * E:(g + 1) * 2 * E], logitsT[k][0:2 * E, rows(g % 4)],
                                      cst[0:2 * E, C_IDENT:C_IDENT + 2 * E])
                ins.then_inc(logits_done, 1)

            pe.wait_ge(zero_ok, 1)
            keep_warm(10)
            for k in range(KC):
                embed(0, k)
            for k in range(3):
                embed(1, k)
            pe.wait_ge(wsm_ok, 1)
            second_layer(0)
            for k in range(3, KC):
                embed(1, k)
            pe.wait_ge(cst_in, 32)
            keep_warm(10, 0)
            transpose_xn(0)
            keep_warm(2, 4)
            second_layer(1)
            pe.wait_ge(wsm_ok, 5)
            b_proj(0)
            gate_proj(0, 0)
            gate_proj(0, 1)
            c_proj(0)
            keep_warm(3, 6)
            transpose_xn(1)
            keep_warm(3, 6)
            b_proj(1)
            gate_proj(1, 0)
            turn_back(0)
            gate_proj(1, 1)
            c_proj(1)
            keep_warm(8, 0)
            transpose_xn(2)
            keep_warm(8, 4)
            turn_back(1)
            pe.wait_ge(rw1_ok, 1)
            router(0)
            router(1)
            router(2)
            logits(0)
            router(3)
            logits(1)
            transpose_xn(3)
            logits(2)
            router(4)
            logits(3)
            router(5, lambda: turn_logits(0))
            router(6)
            pe.wait_ge(mask_a_ok, 1)
            T.matmul(bank[7][:, 0:E], cst[:, C_TRI:C_TRI + P], incl[:, 0, :, GH - 1], start=True, stop=True)
            T.matmul(bank[7][:, E:2 * E], cst[:, C_ONES:C_ONES + P], incl[:, 0, :, GH - 1], start=True,
                     stop=True).then_inc(counts_a_done, 1)
            router(7)
            logits(4)
            keep_warm(8, 3)
            for a in range(2 * GH):
                pe.wait_ge(onehot_a_ok, a // GH + 1)
                ins = T.matmul(bank[0][:, 0:NAP], ohlo_a[:, a, :], tabrhs_a[:, a, :], start=a == 0, stop=a == 2 * GH - 1)
            ins.then_inc(table_a_done, 1)
            logits(5)
            logits(6)
            logits(7)
            turn_logits(1)
            keep_warm(8, 3)

            def second_counts():
                pe.wait_ge(mask_ok, 1)
                T.matmul(bank[2][:, 0:E], cst[:, C_TRI:C_TRI + P], incl[:, 1, :, GH - 1], start=True, stop=True)
                T.matmul(bank[2][:, E:2 * E], cst[:, C_ONES:C_ONES + P], incl[:, 0, :, GH - 1], start=True, stop=False)
                T.matmul(bank[2][:, E:2 * E], cst[:, C_ONES:C_ONES + P], incl[:, 1, :, GH - 1], start=False,
                         stop=True).then_inc(counts_done, 1)

            def second_table():
                for a in range(2 * G):
                    pe.wait_ge(onehot_ok, 2 * a // G + 1)
                    pe.wait_ge(told_ok, a // G + 1)
                    ins = T.matmul(bank[2][:, 0:3 * NTP], oh_lo[:, a, :],
                                   tab_rhs[:, a].rearrange("p k j -> p (k j)"), start=a == 0, stop=a == 2 * G - 1)
                ins.then_inc(table_done, 1)

            def turn_in(j, par, count):
                pe.wait_ge(gathered[par], 16 * count)
                if not isinstance(j, int) or j >= 1:
                    pe.wait_ge(xg_ok, j)
                for c in range(DC):
                    ins = T.transpose(bank[3][:, c * P:(c + 1) * P], xg[:, par, c * P:(c + 1) * P], ident)
                ins.then_inc(xgT_done, 1)

            def up_proj(i, par, first):
                e = pe.value_load(e_of_tile[0:1, bass.ds(i, 1)], min_val=0, max_val=E - 1)
                pe.wait_ge(xg_ok, i + 1)
                for n in range(2):
                    if not first:
                        pe.wait_ge(hpre_ok, 2 * i - 1 + n)
                    hs = slice(n * 512, (n + 1) * 512)
                    for c in range(DC):
                        w_hi = w1e_hi[:, bass.ds(e, 1), c, hs].squeeze(1)
                        w_lo = w1e_lo[:, bass.ds(e, 1), c, hs].squeeze(1)
                        ins = three(bank[4 + n][:, :], xg_hi[:, par, c, :], xg_lo[:, par, c, :], w_hi, w_lo,
                                    c == 0, c == DC - 1)
                    ins.then_inc(up_done, 1)
                    if first and n == 0:
                        turn_in(1, 1, 1)

            def turn(j, par, first):
                for n in range(2):
                    pe.wait_ge(hpre_ok, 2 * j + n + 1)
                    if not first:
                        pe.wait_ge(gelu_ok, 2 * j - 1 + n)
                    for c in range(4):
                        hc = 4 * n + c
                        ins = T.transpose(bank[6 + n][:, rows(c)], hpre[:, par, hc * P:(hc + 1) * P], ident)
                    ins.then_inc(hT_done, 1)

            def down_proj(j, par, first):
                e = pe.value_load(e_of_tile[0:1, bass.ds(j, 1)], min_val=0, max_val=E - 1)
                if not first:
                    pe.wait_ge(y_ok, j - 1)
                for hc in range(HC):
                    if hc % 4 == 0:
                        pe.wait_ge(hT_ok, 2 * j + hc // 4 + 1)
                    w_hi = w2e_hi[:, bass.ds(e, 1), hc, :].squeeze(1)
                    w_lo = w2e_lo[:, bass.ds(e, 1), hc, :].squeeze(1)
                    ins = three(bank[par][:, 0:D], hT_hi[:, par, hc, :], hT_lo[:, par, hc, :], w_hi, w_lo,
                                hc == 0, hc == HC - 1)
                ins.then_inc(down_done, 1)

            pe.wait_ge(emap_a_ok, 1)
            turn_in(0, 0, 1)
            keep_warm(4, 7)
            pe.wait_ge(w1e_ok, DC * E)
            for i in range(4):
                up_proj(i, i % 2, i == 0)
                if i == 0:
                    second_counts()
                if i >= 1:
                    turn_in(i + 1, (i + 1) % 2, (i + 1) // 2 + 1)
                if i >= 1:
                    turn(i - 1, (i - 1) % 2, i - 1 == 0)
                if i == 2:
                    pe.wait_ge(w2e_ok, 2 * (E - 1))
                    pe.wait_ge(w2e_last_ok, 2)
                if i == 3:
                    second_table()
                if i >= 2:
                    down_proj(i - 2, i % 2, i - 2 < 2)
            pe.wait_ge(emap_ok, 1)
            with pe.Fori(FULL.start // 2, FULL.stop // 2) as m:
                for par in range(2):
                    i = 2 * m + par
                    up_proj(i, par, False)
                    turn_in(i + 1, 1 - par, m + 1 + par)
                    turn(i - 1, 1 - par, False)
                    down_proj(i - 2, par, False)
            for i in range(FULL.stop, NT + 2):
                if i < NT:
                    up_proj(i, i % 2, False)
                if i - 1 < NT:
                    turn(i - 1, (i - 1) % 2, False)
                down_proj(i - 2, i % 2, False)


def kernel(**inputs):
    import numpy as np
    import concourse.bacc as bacc
    from concourse import mybir as mb
    from concourse.bass_utils import run_bass_kernel_spmd

    a = {k.replace("L0_", ""): np.asarray(v) for k, v in inputs.items()}
    gh = 4
    xT = a["x"].reshape(64, 3, gh, 16, gh, 16).transpose(1, 3, 5, 0, 2, 4).reshape(KC, P, TOKENS)

    def cols(v):
        return v.reshape(-1, P).T

    vecs = np.concatenate([cols(a["tok_b1"]), cols(a["attn_gate_b"]), cols(a["attn_log_decay"]), cols(a["ffn_rb1"]),
                           a["ffn_rW2"].reshape(RC, P, E).transpose(1, 0, 2).reshape(P, RC * E)], axis=1)
    p = np.arange(P)
    one = np.ones((P, 1))
    e = np.arange(E)
    consts = np.concatenate([
        np.eye(P), one * p, p[:, None] < p[None, :], np.ones((P, P)), 
        one * np.arange(NTP), one * (P * np.arange(G)), p[:, None] + P * np.arange(G) + 1, p[:, None] + TOKENS + 1,
        one * np.stack([e[None, :] > e[:, None], e[None, :] < e[:, None]], axis=1).reshape(1, -1),
        one * (np.arange(E * G // 2) % (G // 2) != 0), np.full((P, G), -0.5)], axis=1).astype(np.float32)
    arrays = {
        "xT": xT, "w1": a["tok_W1"], "w2": a["tok_W2"], "b2": a["tok_b2"], "bw": a["attn_B_w"].T, "cw": a["attn_C_w"].T,
        "gw": a["attn_gate_w"].T, "rw1": a["ffn_rW1"], "rb2": a["ffn_rb2"], "we1": a["ffn_We1"], "be1": a["ffn_be1"],
        "we2": a["ffn_We2"], "be2": a["ffn_be2"], "vecs": vecs, "consts": consts,
    }
    arrays = {k: np.ascontiguousarray(v) for k, v in arrays.items()}
    nc = bacc.Bacc("TRN2", target_bir_lowering=False, num_devices=1)
    aps = {k: nc.dram_tensor(f"in_{k}", v.shape, mb.dt.from_np(v.dtype), kind="ExternalInput").ap()
           for k, v in arrays.items()}
    out = nc.dram_tensor("out_rows", (TOKENS + P, D), mb.dt.float32, kind="ExternalOutput").ap()
    tower(nc, *(aps[k] for k in arrays), out)
    r = run_bass_kernel_spmd(nc, [{f"in_{k}": v for k, v in arrays.items()}], core_ids=[0])
    return r.results[0]["out_rows"][:TOKENS].reshape(64, SEQ, D)
```
